# Optimizing a Trainium2 kernel written in Bass

```python
import numpy as np
import jax
import jax.numpy as jnp

def _softmax(x, axis=-1):
    return jax.nn.softmax(x, axis=axis)

def _gelu(x):
    return jax.nn.gelu(x, approximate=True)

def _silu(x):
    return jax.nn.silu(x)

def _sigmoid(x):
    return jax.nn.sigmoid(x)

def _layernorm(x, axis=-1, eps=1e-05):
    m = jnp.mean(x, axis=axis, keepdims=True)
    v = jnp.var(x, axis=axis, keepdims=True)
    return (x - m) / jnp.sqrt(v + eps)

def _scatter_add(tgt, idx, src, axis=0):
    return tgt.at[idx].add(src)

def _segment_sum(src, seg, n):
    return jax.ops.segment_sum(src, seg, n)
kernel_name = 'mk_prb_d2_jaxref_r8_f4cc2d'

def setup_inputs(seed: int=0):
    np.random.seed(seed)
    _w = jnp.asarray

    def _L0_attn_setup():
        import jax, jax.numpy as jnp
        import numpy as np
        B, S, HID = (1, 256, 512)
        H, NOPE, ROPE, VD = (32, 128, 64, 128)
        QKD = NOPE + ROPE
        Q_RANK, KV_RANK = (192, 64)
        IDX_H, IDX_D, TOPK = (16, 128, 128)
        EPS, THETA = (1e-05, 10000.0)

        def rmsnorm(x, w):
            return x * jax.lax.rsqrt(jnp.mean(x * x, axis=-1, keepdims=True) + EPS) * w

        def rope_interleaved(x, pos):
            d = x.shape[-1]
            inv_freq = 1.0 / THETA ** (jnp.arange(0, d, 2, dtype=jnp.float32) / d)
            ang = pos[:, None] * inv_freq[None, :]
            cos, sin = (jnp.cos(ang), jnp.sin(ang))
            x2 = x.reshape(*x.shape[:-1], d // 2, 2)
            x0, x1 = (x2[..., 0], x2[..., 1])
            return jnp.stack([x0 * cos - x1 * sin, x1 * cos + x0 * sin], axis=-1).reshape(x.shape)
        key = jax.random.key(seed)
        ks = jax.random.split(key, 12)
        s = 0.02
        return {'hidden_states': jax.random.normal(ks[0], (B, S, HID), jnp.float32), 'q_a_w': jax.random.normal(ks[1], (HID, Q_RANK), jnp.float32) * s, 'q_a_norm_w': jnp.ones((Q_RANK,), jnp.float32), 'q_b_w': jax.random.normal(ks[2], (Q_RANK, H * QKD), jnp.float32) * s, 'kv_a_w': jax.random.normal(ks[3], (HID, KV_RANK + ROPE), jnp.float32) * s, 'kv_a_norm_w': jnp.ones((KV_RANK,), jnp.float32), 'kv_b_w': jax.random.normal(ks[4], (KV_RANK, H * (NOPE + VD)), jnp.float32) * s, 'o_w': jax.random.normal(ks[5], (H * VD, HID), jnp.float32) * s, 'idx_wq_w': jax.random.normal(ks[6], (HID, IDX_H * IDX_D), jnp.float32) * s, 'idx_wk_w': jax.random.normal(ks[7], (HID, IDX_D), jnp.float32) * s, 'idx_weights_w': jax.random.normal(ks[8], (HID, IDX_H), jnp.float32) * s}
    _L0_attn_in = _L0_attn_setup()

    def _L0_ffn_setup():
        import jax, jax.numpy as jnp
        import numpy as np
        DIM = 512
        HID = 1376
        R = 16
        SCALING = 32.0 / 16.0

        def _lora_linear(x, w, a, b):
            base = jnp.einsum('bsd,od->bso', x, w)
            low = jnp.einsum('bsr,or->bso', jnp.einsum('bsd,rd->bsr', x, a), b)
            return base + low * SCALING
        key = jax.random.key(seed)
        ks = jax.random.split(key, 10)
        s_in = 1.0 / np.sqrt(DIM)
        s_hid = 1.0 / np.sqrt(HID)
        return {'x': jax.random.normal(ks[0], (4, 256, DIM), jnp.float32), 'w1': jax.random.normal(ks[1], (HID, DIM), jnp.float32) * s_in, 'w3': jax.random.normal(ks[2], (HID, DIM), jnp.float32) * s_in, 'w2': jax.random.normal(ks[3], (DIM, HID), jnp.float32) * s_hid, 'lora_A1': jax.random.normal(ks[4], (R, DIM), jnp.float32) * s_in, 'lora_B1': jax.random.normal(ks[5], (HID, R), jnp.float32) * 0.02, 'lora_A3': jax.random.normal(ks[6], (R, DIM), jnp.float32) * s_in, 'lora_B3': jax.random.normal(ks[7], (HID, R), jnp.float32) * 0.02, 'lora_A2': jax.random.normal(ks[8], (R, HID), jnp.float32) * s_hid, 'lora_B2': jax.random.normal(ks[9], (DIM, R), jnp.float32) * 0.02}
    _L0_ffn_in = _L0_ffn_setup()

    def _L1_attn_setup():
        import jax, jax.numpy as jnp
        import numpy as np
        B, T, D = (1, 256, 512)
        H, G = (32, 8)
        HD = D // H
        REP = H // G
        KV_DIM = 2 * HD * G
        key = jax.random.key(seed)
        k0, k1, k2, k3 = jax.random.split(key, 4)
        x = jax.random.normal(k0, (B, T, D), dtype=jnp.float32)
        Wq = jax.random.normal(k1, (D, D), dtype=jnp.float32) * 0.02
        Wkv = jax.random.normal(k2, (D, KV_DIM), dtype=jnp.float32) * 0.02
        Wo = jax.random.normal(k3, (D, D), dtype=jnp.float32) * 0.02
        bo = jnp.zeros((D,), dtype=jnp.float32)
        return {'x': x, 'Wq': Wq, 'Wkv': Wkv, 'Wo': Wo, 'bo': bo}
    _L1_attn_in = _L1_attn_setup()

    def _L1_ffn_setup():
        import jax, jax.numpy as jnp
        import numpy as np
        B, S, D, F = (4, 256, 512, 2048)
        key = jax.random.key(seed)
        k = jax.random.split(key, 5)
        scale_in = 1.0 / np.sqrt(D)
        scale_out = 1.0 / np.sqrt(F)
        return {'input': jax.random.normal(k[0], (B, S, D), dtype=jnp.float32), 'inter_w': jax.random.normal(k[1], (D, F), dtype=jnp.float32) * scale_in, 'inter_b': jax.random.normal(k[2], (F,), dtype=jnp.float32) * 0.02, 'output_w': jax.random.normal(k[3], (F, D), dtype=jnp.float32) * scale_out, 'output_b': jax.random.normal(k[4], (D,), dtype=jnp.float32) * 0.02}
    _L1_ffn_in = _L1_ffn_setup()
    _d = {'L0_attn_hidden_states': _L0_attn_in['hidden_states'], 'L0_attn_q_a_w': _L0_attn_in['q_a_w'], 'L0_attn_q_a_norm_w': _L0_attn_in['q_a_norm_w'], 'L0_attn_q_b_w': _L0_attn_in['q_b_w'], 'L0_attn_kv_a_w': _L0_attn_in['kv_a_w'], 'L0_attn_kv_a_norm_w': _L0_attn_in['kv_a_norm_w'], 'L0_attn_kv_b_w': _L0_attn_in['kv_b_w'], 'L0_attn_o_w': _L0_attn_in['o_w'], 'L0_attn_idx_wq_w': _L0_attn_in['idx_wq_w'], 'L0_attn_idx_wk_w': _L0_attn_in['idx_wk_w'], 'L0_attn_idx_weights_w': _L0_attn_in['idx_weights_w'], 'L0_ffn_w1': _L0_ffn_in['w1'], 'L0_ffn_w3': _L0_ffn_in['w3'], 'L0_ffn_w2': _L0_ffn_in['w2'], 'L0_ffn_lora_A1': _L0_ffn_in['lora_A1'], 'L0_ffn_lora_B1': _L0_ffn_in['lora_B1'], 'L0_ffn_lora_A3': _L0_ffn_in['lora_A3'], 'L0_ffn_lora_B3': _L0_ffn_in['lora_B3'], 'L0_ffn_lora_A2': _L0_ffn_in['lora_A2'], 'L0_ffn_lora_B2': _L0_ffn_in['lora_B2'], 'L1_attn_Wq': _L1_attn_in['Wq'], 'L1_attn_Wkv': _L1_attn_in['Wkv'], 'L1_attn_Wo': _L1_attn_in['Wo'], 'L1_attn_bo': _L1_attn_in['bo'], 'L1_ffn_inter_w': _L1_ffn_in['inter_w'], 'L1_ffn_inter_b': _L1_ffn_in['inter_b'], 'L1_ffn_output_w': _L1_ffn_in['output_w'], 'L1_ffn_output_b': _L1_ffn_in['output_b']}
    _x0 = _d['L0_attn_hidden_states']
    _d['L0_attn_hidden_states'] = jax.random.normal(jax.random.fold_in(jax.random.key(seed), 1), (1, 1024, 512), dtype=_x0.dtype)
    del _x0
    return _d

def reference(L0_attn_hidden_states, L0_attn_q_a_w, L0_attn_q_a_norm_w, L0_attn_q_b_w, L0_attn_kv_a_w, L0_attn_kv_a_norm_w, L0_attn_kv_b_w, L0_attn_o_w, L0_attn_idx_wq_w, L0_attn_idx_wk_w, L0_attn_idx_weights_w, L0_ffn_w1, L0_ffn_w3, L0_ffn_w2, L0_ffn_lora_A1, L0_ffn_lora_B1, L0_ffn_lora_A3, L0_ffn_lora_B3, L0_ffn_lora_A2, L0_ffn_lora_B2, L1_attn_Wq, L1_attn_Wkv, L1_attn_Wo, L1_attn_bo, L1_ffn_inter_w, L1_ffn_inter_b, L1_ffn_output_w, L1_ffn_output_b):

    def _L0_attn_ref(hidden_states, q_a_w, q_a_norm_w, q_b_w, kv_a_w, kv_a_norm_w, kv_b_w, o_w, idx_wq_w, idx_wk_w, idx_weights_w):
        import jax, jax.numpy as jnp
        import numpy as np
        B, S, HID = (1, 256, 512)
        H, NOPE, ROPE, VD = (32, 128, 64, 128)
        QKD = NOPE + ROPE
        Q_RANK, KV_RANK = (192, 64)
        IDX_H, IDX_D, TOPK = (16, 128, 128)
        EPS, THETA = (1e-05, 10000.0)

        def rmsnorm(x, w):
            return x * jax.lax.rsqrt(jnp.mean(x * x, axis=-1, keepdims=True) + EPS) * w

        def rope_interleaved(x, pos):
            d = x.shape[-1]
            inv_freq = 1.0 / THETA ** (jnp.arange(0, d, 2, dtype=jnp.float32) / d)
            ang = pos[:, None] * inv_freq[None, :]
            cos, sin = (jnp.cos(ang), jnp.sin(ang))
            x2 = x.reshape(*x.shape[:-1], d // 2, 2)
            x0, x1 = (x2[..., 0], x2[..., 1])
            return jnp.stack([x0 * cos - x1 * sin, x1 * cos + x0 * sin], axis=-1).reshape(x.shape)
        b, s, _ = hidden_states.shape
        pos = jnp.arange(s, dtype=jnp.float32)
        q_lat = rmsnorm(hidden_states @ q_a_w, q_a_norm_w)
        q = (q_lat @ q_b_w).reshape(b, s, H, QKD).transpose(0, 2, 1, 3)
        q_nope, q_pe = (q[..., :NOPE], q[..., NOPE:])
        ckv = hidden_states @ kv_a_w
        kv_lat, k_pe = (ckv[..., :KV_RANK], ckv[..., KV_RANK:])
        kv = (rmsnorm(kv_lat, kv_a_norm_w) @ kv_b_w).reshape(b, s, H, NOPE + VD).transpose(0, 2, 1, 3)
        k_nope, v = (kv[..., :NOPE], kv[..., NOPE:])
        q_pe = rope_interleaved(q_pe, pos)
        k_pe = rope_interleaved(k_pe[:, None, :, :], pos)
        scores = (jnp.einsum('bhqd,bhkd->bhqk', q_nope, k_nope) + jnp.einsum('bhqd,bhkd->bhqk', q_pe, k_pe)) * QKD ** (-0.5)
        iq = (hidden_states @ idx_wq_w).reshape(b, s, IDX_H, IDX_D)
        ik = hidden_states @ idx_wk_w
        iw = hidden_states @ idx_weights_w * IDX_H ** (-0.5)
        idx_scores = jnp.einsum('bqn,bnqk->bqk', iw, jax.nn.relu(jnp.einsum('bqnd,bkd->bnqk', iq, ik))) * IDX_D ** (-0.5)
        causal = pos[:, None] >= pos[None, :]
        idx_scores = jnp.where(causal, idx_scores, -jnp.inf)
        _, topk_idx = jax.lax.top_k(idx_scores, TOPK)
        bi = jnp.arange(b)[:, None, None]
        qi = jnp.arange(s)[None, :, None]
        topk_mask = jnp.zeros((b, s, s), bool).at[bi, qi, topk_idx].set(True)
        mask = topk_mask & causal
        scores = jnp.where(mask[:, None], scores, -jnp.inf)
        attn = jax.nn.softmax(scores, axis=-1)
        out = jnp.einsum('bhqk,bhkd->bqhd', attn, v).reshape(b, s, H * VD)
        return out @ o_w

    def _L0_ffn_ref(x, w1, w3, w2, lora_A1, lora_B1, lora_A3, lora_B3, lora_A2, lora_B2):
        import jax, jax.numpy as jnp
        import numpy as np
        DIM = 512
        HID = 1376
        R = 16
        SCALING = 32.0 / 16.0

        def _lora_linear(x, w, a, b):
            base = jnp.einsum('bsd,od->bso', x, w)
            low = jnp.einsum('bsr,or->bso', jnp.einsum('bsd,rd->bsr', x, a), b)
            return base + low * SCALING
        h1 = _lora_linear(x, w1, lora_A1, lora_B1)
        h3 = _lora_linear(x, w3, lora_A3, lora_B3)
        g = jax.nn.silu(h1) * h3
        return _lora_linear(g, w2, lora_A2, lora_B2)

    def _L1_attn_ref(x, Wq, Wkv, Wo, bo):
        import jax, jax.numpy as jnp
        import numpy as np
        B, T, D = (1, 256, 512)
        H, G = (32, 8)
        HD = D // H
        REP = H // G
        KV_DIM = 2 * HD * G
        b, t, d = x.shape
        q = jnp.dot(x, Wq).reshape(b, t, H, HD).transpose(0, 2, 1, 3)
        kv = jnp.dot(x, Wkv).reshape(b, t, G, 2, HD).transpose(2, 3, 0, 1, 4)
        k, v = (kv[:, 0], kv[:, 1])
        k = jnp.broadcast_to(k[:, :, None], (G, b, REP, t, HD)).reshape(b, H, t, HD)
        v = jnp.broadcast_to(v[:, :, None], (G, b, REP, t, HD)).reshape(b, H, t, HD)
        scores = jnp.einsum('bhqd,bhkd->bhqk', q, k)
        causal = jnp.triu(jnp.ones((t, t), dtype=bool), 1)
        scores = jnp.where(causal[None, None], -jnp.inf, scores)
        weights = jax.nn.softmax(scores * (1.0 / HD ** 0.5), axis=-1)
        ctx = jnp.einsum('bhqk,bhkd->bhqd', weights, v)
        ctx = ctx.transpose(0, 2, 1, 3).reshape(b, t, d)
        return jnp.dot(ctx, Wo) + bo

    def _L1_ffn_ref(input, inter_w, inter_b, output_w, output_b):
        import jax, jax.numpy as jnp
        import numpy as np
        B, S, D, F = (4, 256, 512, 2048)
        h = jax.nn.gelu(jnp.einsum('bsd,df->bsf', input, inter_w) + inter_b, approximate=True)
        out = jnp.einsum('bsf,fd->bsd', h, output_w) + output_b
        return out
    x = L0_attn_hidden_states
    xn = _layernorm(x, axis=-1)
    x = x + _L0_attn_ref(xn, L0_attn_q_a_w, L0_attn_q_a_norm_w, L0_attn_q_b_w, L0_attn_kv_a_w, L0_attn_kv_a_norm_w, L0_attn_kv_b_w, L0_attn_o_w, L0_attn_idx_wq_w, L0_attn_idx_wk_w, L0_attn_idx_weights_w) + _L0_ffn_ref(xn, L0_ffn_w1, L0_ffn_w3, L0_ffn_w2, L0_ffn_lora_A1, L0_ffn_lora_B1, L0_ffn_lora_A3, L0_ffn_lora_B3, L0_ffn_lora_A2, L0_ffn_lora_B2)
    xn = _layernorm(x, axis=-1)
    x = x + _L1_attn_ref(xn, L1_attn_Wq, L1_attn_Wkv, L1_attn_Wo, L1_attn_bo) + _L1_ffn_ref(xn, L1_ffn_inter_w, L1_ffn_inter_b, L1_ffn_output_w, L1_ffn_output_b)
    return x

_drawn_inputs = setup_inputs


def setup_inputs(seed=0):
    import zlib

    import numpy as np

    out = dict(_drawn_inputs(seed))
    spreads = {'L0_attn_q_a_norm_w': (1.0, 0.6),
     'L0_attn_kv_a_norm_w': (1.0, 0.6),
     'L1_attn_bo': (0.0, 0.312)}
    factors = {'L0_attn_q_a_w': 8.0,
     'L0_attn_q_b_w': 8.0,
     'L0_attn_kv_a_w': 2.919,
     'L0_attn_kv_b_w': 2.932,
     'L0_attn_o_w': 2.866,
     'L0_attn_idx_wq_w': 4.191,
     'L0_attn_idx_wk_w': 4.162,
     'L0_attn_idx_weights_w': 4.189,
     'L1_attn_Wq': 8.0,
     'L1_attn_Wkv': 4.446,
     'L1_attn_Wo': 4.559,
     'L1_ffn_inter_b': 6.127,
     'L1_ffn_output_b': 4.275}
    for name, (base, spread) in spreads.items():
        noise = np.random.default_rng([zlib.crc32(name.encode()), seed]).standard_normal(out[name].shape)
        drawn = base * np.exp(spread * noise) if base else spread * noise
        out[name] = jnp.asarray(drawn.astype(out[name].dtype))
    for name, factor in factors.items():
        out[name] = (out[name] * factor).astype(out[name].dtype)
    return out
```

```python
from contextlib import ExitStack

import numpy as np
import concourse.bass as bass
from concourse import mybir

F32 = mybir.dt.float32
F32R = mybir.dt.float32r
BF16 = mybir.dt.bfloat16
ALU = mybir.AluOpType
ACT = mybir.ActivationFunctionType
AX_X = mybir.AxisListType.X

P = 128
S = 1024
D = 512
ST = S // P
DT = D // P
HALF = 512
PAIR = 2 * P
EPS = 1e-5

H = 32
NOPE, ROPE, VD = 128, 64, 128
QKD = NOPE + ROPE
QR, KVR = 192, 64
QC = QR // 2
IH, ID, TOPK = 16, 128, 128
LAT = QR + KVR + ROPE + ID + IH
C_KV, C_PE, C_IK, C_IW = QR, QR + KVR, QR + KVR + ROPE, QR + KVR + ROPE + ID

F0, R0 = 1376, 16
LORA_SCALE = 2.0
F1 = 2048
G1, HD1 = 8, 16
REP1 = H // G1

MASKED = -1.0e30
TAKEN = -3.0e38
MASK_OFF = [P * t * (t + 1) // 2 for t in range(ST + 1)]


def f32(ap):
    return ap.bitcast(F32)


class Ctx:

    def __init__(self, nc, stack):
        self.nc, self.stack, self.mine = nc, stack, []

    def sb(self, name, shape, dt=F32):
        return self.stack.enter_context(self.nc.sbuf_tensor(name, shape, dt))

    def sem(self, name):
        s = self.stack.enter_context(self.nc.semaphore(name))
        self.mine.append(s)
        return s

    def sems(self, name, n):
        return [self.sem(f"{name}{i}") for i in range(n)]

    def clear(self):
        with self.nc.Block() as block:
            @block.gpsimd
            def _(pool):
                for s in self.mine:
                    pool.sem_clear(s)


def pause(eng, sem, value, passed):
    eng.wait_ge(sem, value)
    eng.sem_inc(passed, 1)


def mm3(pe, out, left, right, start, stop):
    (lh, ll), (rh, rl) = left, right
    pe.matmul(out, lh, rh, start=start, stop=False, skip_group_check=True)
    pe.matmul(out, lh, rl, start=False, stop=False, skip_group_check=True)
    return pe.matmul(out, ll, rh, start=False, stop=stop, skip_group_check=True)


def fold_attention_weights(nc, ps, ident, q_b_w, kv_b_w, o_w, wabs_d, wvo_d):
    NP = H // 2
    with ExitStack() as st:
        c = Ctx(nc, st)
        wq = c.sb("fw_wq", [QC, 2, 2, QKD])
        wkv = c.sb("fw_wkv", [KVR, 2, NOPE + VD])
        wo = c.sb("fw_wo", [P, 2, D])
        wT = c.sb("fw_wT", [P, 2, 320])
        wabs = c.sb("fw_wabs", [QC, 2, 3, P])
        wvo = c.sb("fw_wvo", [P, D])
        passed = c.sem("fw_passed")
        raw_in, turned, wT_done, folded, abs_done, vo_done, pe_copied, stored = (
            c.sem(n) for n in ("fw_raw_in", "fw_turned", "fw_wT_done", "fw_folded", "fw_abs_done",
                               "fw_vo_done", "fw_pe_copied", "fw_stored"))
        wq_v = q_b_w.rearrange("(c p) (j a n) -> j p c a n", c=2, a=2, n=QKD)
        wkv_v = kv_b_w.rearrange("p (j a n) -> j p a n", a=2, n=NOPE + VD)
        wo_v = o_w.rearrange("(j a p) n -> j p a n", a=2, p=VD)
        with nc.Block() as block:
            @block.sync
            def _(sp):
                with sp.Fori(0, NP) as i:
                    sp.wait_ge(folded, i * 2)
                    sp.wait_ge(pe_copied, i)
                    for c_ in range(2):
                        sp.dma_start(wq[:, c_], wq_v[i][:, c_]).then_inc(raw_in, 16)
                    sp.dma_start(wkv[:, :, :], wkv_v[i]).then_inc(raw_in, 16)
                    sp.dma_start(wo[:, :, :], wo_v[i]).then_inc(raw_in, 16)
                    sp.wait_ge(abs_done, i + 1)
                    sp.wait_ge(pe_copied, i + 1)
                    sp.dma_start(wabs_d[i], wabs[:, :, :, :].rearrange("p c b n -> p (c b n)")).then_inc(stored, 16)
                    sp.wait_ge(vo_done, i + 1)
                    sp.dma_start(wvo_d[i], wvo[:, :]).then_inc(stored, 16)
                sp.wait_ge(stored, 32 * NP)

            @block.tensor
            def _(pe):
                with pe.Fori(0, NP) as i:
                    pe.wait_ge(raw_in, i * 64 + 64)
                    pe.wait_ge(wT_done, i * 2)
                    for a in range(2):
                        for k in range(2):
                            pe.transpose(ps[:, a, k * QC:(k + 1) * QC], wq[:, k, a, 0:NOPE], ident[0:QC, 0:QC])
                        pe.transpose(ps[:, a, 192:256], wkv[:, a, 0:NOPE], ident[0:KVR, 0:KVR])
                        pe.transpose(ps[:, a, 256:320], wkv[:, a, NOPE:], ident[0:KVR, 0:KVR]).then_inc(turned, 1)
                    pe.wait_ge(abs_done, i)
                    pe.wait_ge(vo_done, i)
                    pe.wait_ge(wT_done, i * 2 + 2)
                    for a in range(2):
                        for k in range(2):
                            pe.matmul(ps[0:QC, 2, (a * 2 + k) * 64:(a * 2 + k + 1) * 64],
                                      wT[:, a, k * QC:(k + 1) * QC], wT[:, a, 192:256], start=True, stop=True)
                        pe.matmul(ps[64 * a:64 * a + 64, 3 + a, :], wT[:, a, 256:320], wo[:, a, :],
                                  start=True, stop=True).then_inc(folded, 1)

            @block.scalar
            def _(act):
                with act.Fori(0, NP) as i:
                    for a in range(2):
                        act.wait_ge(turned, i * 2 + a + 1)
                        if a == 0:
                            act.wait_ge(folded, i * 2)
                        act.copy(wT[:, a, :], ps[:, a, 0:320]).then_inc(wT_done, 1)
                    act.wait_ge(folded, i * 2 + 2)
                    act.wait_ge(stored, i * 32)
                    for a in range(2):
                        ins = act.copy(wvo[64 * a:64 * a + 64, :], ps[64 * a:64 * a + 64, 3 + a, :])
                    ins.then_inc(vo_done, 1)

            @block.vector
            def _(dve):
                with dve.Fori(0, NP) as i:
                    dve.wait_ge(folded, i * 2 + 2)
                    dve.wait_ge(stored, i * 32)
                    for a in range(2):
                        ins = dve.tensor_copy(wabs[:, :, a, 0:64],
                                              ps[0:QC, 2, a * 128:(a + 1) * 128].rearrange("p (k n) -> p k n", k=2))
                    ins.then_inc(abs_done, 1)

            @block.gpsimd
            def _(pool):
                with pool.Fori(0, NP) as i:
                    pool.wait_ge(raw_in, i * 64 + 64)
                    pause(pool, stored, i * 32, passed)
                    for a in range(2):
                        pair = wq[:, :, a, NOPE:].rearrange("p c (n e) -> p c e n", e=2)
                        pool.tensor_copy(wabs[:, :, a, 64:96], pair[:, :, 0, :])
                        pool.tensor_copy(wabs[:, :, a, 96:128], pair[:, :, 1, :])
                        pool.tensor_copy(wabs[:, :, 2, 64 * a:64 * a + 32], pair[:, :, 1, :])
                        ins = pool.tensor_copy(wabs[:, :, 2, 64 * a + 32:64 * a + 64], pair[:, :, 0, :])
                    ins.then_inc(pe_copied, 1)
        c.clear()


def fold_lora(nc, ps, ident, w1, w3, w2, A1, B1, A3, B3, A2, B2, w1T_d, w3T_d, w2T_d):
    NF = F0 // P
    LASTN = F0 - NF * P
    with ExitStack() as st:
        c = Ctx(nc, st)
        wr = c.sb("fl_w", [P, 2, D])
        w2r = c.sb("fl_w2", [P, DT, P])
        br = c.sb("fl_b", [P, 2, R0])
        a13 = c.sb("fl_a13", [R0, 2, D])
        a2 = c.sb("fl_a2", [R0, P])
        b2 = c.sb("fl_b2", [P, DT, R0])
        b2T = c.sb("fl_b2T", [R0, D])
        bT = c.sb("fl_bT", [R0, 2, P])
        wT = c.sb("fl_wT", [P, 2, DT, P])
        w2T = c.sb("fl_w2T", [P, D])
        passed = c.sem("fl_passed")
        once_in, b2_turned, b2_done, raw_in, b_turned, bT_done, summed, evac_a, evac_d, stored = (
            c.sem(n) for n in ("fl_once_in", "fl_b2_turned", "fl_b2_done", "fl_raw_in", "fl_b_turned", "fl_bT_done",
                               "fl_summed", "fl_evac_a", "fl_evac_d", "fl_stored"))
        w1T_v = w1T_d.rearrange("(k p) n -> p k n", p=P)
        w3T_v = w3T_d.rearrange("(k p) n -> p k n", p=P)
        w2_v = w2.rearrange("(k p) n -> p k n", p=P)

        def bank(b):
            return ps[:, b, :].rearrange("p (k n) -> p k n", k=DT)

        def chunks(eng, body):
            with eng.Fori(0, NF) as i:
                body(i, P)
            body(NF, LASTN)

        with nc.Block() as block:
            @block.sync
            def _(sp):
                sp.dma_start(a13[:, 0], A1).then_inc(once_in, 16)
                sp.dma_start(a13[:, 1], A3).then_inc(once_in, 16)
                sp.dma_start(b2[:, :, :], B2.rearrange("(k p) r -> p k r", p=P)).then_inc(once_in, 16)

                def body(i, n):
                    at = bass.ds(i * P, n)
                    sp.wait_ge(summed, i * 3)
                    sp.dma_start(wr[0:n, 0], w1[at, :]).then_inc(raw_in, 16)
                    sp.dma_start(wr[0:n, 1], w3[at, :]).then_inc(raw_in, 16)
                    sp.dma_start(w2r[:, :, 0:n], w2_v[:, :, at]).then_inc(raw_in, 16)
                    sp.dma_start(a2[:, 0:n], A2[:, at]).then_inc(raw_in, 16)
                    sp.dma_start(br[0:n, 0], B1[at, :]).then_inc(raw_in, 16)
                    sp.dma_start(br[0:n, 1], B3[at, :]).then_inc(raw_in, 16)
                    pause(sp, evac_a, i * 2 + 2, passed)
                    sp.wait_ge(evac_d, i + 1)
                    sp.dma_start(w1T_v[:, :, at], wT[:, 0, :, 0:n]).then_inc(stored, 16)
                    sp.dma_start(w3T_v[:, :, at], wT[:, 1, :, 0:n]).then_inc(stored, 16)
                    sp.dma_start(w2T_d[at, :], w2T[0:n, :]).then_inc(stored, 16)
                chunks(sp, body)
                sp.wait_ge(stored, 48 * (NF + 1))

            @block.tensor
            def _(pe):
                pe.wait_ge(once_in, 48)
                for k in range(DT):
                    ins = pe.transpose(ps[0:R0, 0, k * P:(k + 1) * P], b2[:, k, :], ident[:, :])
                ins.then_inc(b2_turned, 1)
                pe.wait_ge(b2_done, 1)

                def body(i, n):
                    pe.wait_ge(raw_in, i * 96 + 96)
                    for m in range(2):
                        ins = pe.transpose(ps[0:R0, 0, m * P:m * P + n], br[0:n, m, :], ident[0:n, 0:n])
                    ins.then_inc(b_turned, 1)
                    pe.wait_ge(bT_done, i + 1)
                    pe.wait_ge(evac_a, i * 2)
                    pe.wait_ge(evac_d, i)
                    for m in range(2):
                        for k in range(DT):
                            o = ps[:, 1 + m, k * P:k * P + n]
                            pe.matmul(o, wr[0:n, m, k * P:(k + 1) * P], ident[0:n, 0:n], start=True, stop=False,
                                      is_transpose=True, skip_group_check=True)
                            ins = pe.matmul(o, a13[:, m, k * P:(k + 1) * P], bT[:, m, 0:n], start=False, stop=True,
                                            skip_group_check=True)
                        ins.then_inc(summed, 1)
                    for k in range(DT):
                        o = ps[0:n, 3, k * P:(k + 1) * P]
                        pe.matmul(o, w2r[:, k, 0:n], ident[:, :], start=True, stop=False,
                                  is_transpose=True, skip_group_check=True)
                        ins = pe.matmul(o, a2[:, 0:n], b2T[:, k * P:(k + 1) * P], start=False, stop=True,
                                        skip_group_check=True)
                    ins.then_inc(summed, 1)
                chunks(pe, body)

            @block.scalar
            def _(act):
                act.wait_ge(b2_turned, 1)
                act.mul(b2T[:, :], ps[0:R0, 0, :], LORA_SCALE).then_inc(b2_done, 1)

                def body(i, n):
                    act.wait_ge(b_turned, i + 1)
                    act.mul(bT[:, :, 0:n], ps[0:R0, 0, 0:2 * P].rearrange("r (m n) -> r m n", m=2)[:, :, 0:n],
                            LORA_SCALE).then_inc(bT_done, 1)
                    act.wait_ge(stored, i * 48)
                    act.wait_ge(summed, i * 3 + 1)
                    act.copy(wT[:, 0, :, 0:n], bank(1)[:, :, 0:n]).then_inc(evac_a, 1)
                    act.wait_ge(summed, i * 3 + 3)
                    act.copy(w2T[0:n, :], ps[0:n, 3, :]).then_inc(evac_a, 1)
                chunks(act, body)

            @block.vector
            def _(dve):
                def body(i, n):
                    dve.wait_ge(stored, i * 48)
                    dve.wait_ge(summed, i * 3 + 2)
                    dve.tensor_copy(wT[:, 1, :, 0:n], bank(2)[:, :, 0:n]).then_inc(evac_d, 1)
                chunks(dve, body)
        c.clear()


def layernorm(nc, tag, ps, ident, x, xnh, xnl, x_dram=None):
    with ExitStack() as st:
        c = Ctx(nc, st)
        xn = c.sb(tag + "_xn", [P, ST, D])
        stats = c.sb(tag + "_stats", [P, ST, 6])
        mv = c.sb(tag + "_mv", [P, ST, 2])
        std = c.sb(tag + "_std", [P, ST])
        rstd = c.sb(tag + "_rstd", [P, ST])
        x_in, stat, var_done, std_done, rstd_done, xn_done, turned, hi_done = (
            c.sem(f"{tag}_{n}") for n in ("x_in", "stat", "var_done", "std_done", "rstd_done", "xn_done", "turned",
                                          "hi_done"))
        lo_done = c.sems(tag + "_lo_done", 2)
        with nc.Block() as block:
            @block.sync
            def _(sp):
                if x_dram is not None:
                    for t in range(ST):
                        sp.dma_start(x[:, t], x_dram[t * P:(t + 1) * P, :]).then_inc(x_in, 16)

            @block.vector
            def _(dve):
                for t in range(ST):
                    if x_dram is not None:
                        dve.wait_ge(x_in, 16 * ST)
                    dve.bn_stats(stats[:, t], x[:, t]).then_inc(stat, 1)
                dve.wait_ge(stat, ST)
                for t in range(ST):
                    dve.bn_aggr(mv[:, t], stats[:, t]).then_inc(stat, 1)
                dve.wait_ge(stat, 2 * ST)
                dve.tensor_scalar_add(std[:, :], mv[:, :, 1], EPS).then_inc(var_done, 1)
                dve.wait_ge(std_done, 1)
                dve.reciprocal(rstd[:, :], std[:, :]).then_inc(rstd_done, 1)
                dve.wait_ge(rstd_done, 1)
                for t in range(ST):
                    dve.tensor_scalar(xn[:, t], x[:, t], mv[:, t, 0:1], rstd[:, t:t + 1], ALU.subtract,
                                      ALU.mult).then_inc(xn_done, 1)
                for t in range(ST):
                    dve.wait_ge(hi_done, t + 1)
                    at = slice(t * P, (t + 1) * P)
                    dve.tensor_tensor(xnl[:, :, at], bank4(ps, t % 2), f32(xnh[:, :, at]),
                                      ALU.subtract).then_inc(lo_done[t % 2], 1)

            @block.scalar
            def _(act):
                act.wait_ge(var_done, 1)
                act.activation(std[:, :], std[:, :], ACT.Sqrt).then_inc(std_done, 1)
                for t in range(ST):
                    act.wait_ge(turned, t + 1)
                    act.copy(xnh[:, :, t * P:(t + 1) * P], bank4(ps, t % 2)).then_inc(hi_done, 1)

            @block.tensor
            def _(pe):
                for t in range(ST):
                    pe.wait_ge(xn_done, t + 1)
                    if t >= 2:
                        pe.wait_ge(lo_done[t % 2], t // 2)
                    for k in range(DT):
                        ins = pe.transpose(ps[:, t % 2, k * P:(k + 1) * P], xn[:, t, k * P:(k + 1) * P], ident[:, :])
                    ins.then_inc(turned, 1)
        c.clear()


def bank4(ps, b):
    return ps[:, b, :].rearrange("p (k n) -> p k n", k=4)


def latents(nc, ps, ident, xnh, xnl, q_a_w, kv_a_w, wk_w, ww_w, qn_w, kvn_w, rope_t, qlh, qll, kh, kl, vst, ikh, ikl,
            aw, sg):
    with ExitStack() as st:
        c = Ctx(nc, st)
        w = c.sb("la_w", [P, DT, LAT])
        wh = c.sb("la_wh", [P, DT, LAT], F32R)
        wl = c.sb("la_wl", [P, DT, LAT], F32R)
        lat = c.sb("la_lat", [P, ST, LAT])
        sq = c.sb("la_sq", [P, ST, QR + KVR])
        ss = c.sb("la_ss", [P, 2, ST])
        rs = c.sb("la_rs", [P, 2, ST])
        qn = c.sb("la_qn", [P, QR])
        kvn = c.sb("la_kvn", [P, KVR])
        rope = c.sb("la_rope", [P, ST, 2, ROPE // 2])
        ql = c.sb("la_ql", [P, ST, QR])
        kc = c.sb("la_kc", [P, ST, P])
        rot = c.sb("la_rot", [P, 4, ST, ROPE // 2])
        w_in, c_in, wh_done, wl_done, latted, lat_done, dve_step, ss_done, std_done, tok_done, turned, hi_done, vh_done = (
            c.sem("la_" + n) for n in ("w_in", "c_in", "wh_done", "wl_done", "latted", "lat_done", "dve_step",
                                       "ss_done", "std_done", "tok_done", "turned", "hi_done", "vh_done"))
        lo_done = c.sems("la_lo_done", 2)
        with nc.Block() as block:
            @block.sync
            def _(sp):
                for src, c0, n in ((q_a_w, 0, QR), (kv_a_w, C_KV, KVR + ROPE), (wk_w, C_IK, ID), (ww_w, C_IW, IH)):
                    sp.dma_start(w[:, :, c0:c0 + n], src.rearrange("(k p) n -> p k n", p=P)).then_inc(w_in, 16)
                sp.dma_start(qn[:, :], qn_w.partition_broadcast(P)).then_inc(c_in, 16)
                sp.dma_start(kvn[:, :], kvn_w.partition_broadcast(P)).then_inc(c_in, 16)
                sp.dma_start(rope[:, :, :, :], rope_t.rearrange("(t p) e n -> p t e n", p=P)).then_inc(c_in, 16)

            @block.gpsimd
            def _(pool):
                pool.wait_ge(wh_done, 1)
                pool.tensor_tensor(wl[:, :, :], w[:, :, :], f32(wh[:, :, :]), ALU.subtract).then_inc(wl_done, 1)

            @block.tensor
            def _(pe):
                pe.wait_ge(wl_done, 1)
                for t in range(ST):
                    at = slice(t * P, (t + 1) * P)
                    for k in range(DT):
                        ins = mm3(pe, ps[:, t, 0:LAT], (xnh[:, k, at], xnl[:, k, at]), (wh[:, k], wl[:, k]),
                                  k == 0, k == DT - 1)
                    ins.then_inc(latted, 1)
                pe.wait_ge(tok_done, 1)
                for t in range(ST):
                    if t >= 2:
                        pe.wait_ge(lo_done[t % 2], t // 2)
                    b = t % 2
                    pe.transpose(ps[:, b, 0:P], kc[:, t], ident[:, :])
                    pe.transpose(ps[:, b, P:2 * P], lat[:, t, C_IK:C_IK + ID], ident[:, :])
                    for k in range(2):
                        ins = pe.transpose(ps[0:QC, b, (2 + k) * P:(3 + k) * P], ql[:, t, k * QC:(k + 1) * QC],
                                           ident[:, :])
                    ins.then_inc(turned, 1)

            @block.scalar
            def _(act):
                act.wait_ge(w_in, 64)
                act.copy(wh[:, :, :], w[:, :, :]).then_inc(wh_done, 1)
                for t in range(ST):
                    act.wait_ge(latted, t + 1)
                    act.copy(lat[:, t], ps[:, t, 0:LAT]).then_inc(lat_done, 1)
                act.wait_ge(ss_done, 1)
                act.activation(ss[:, :, :], ss[:, :, :], ACT.Sqrt).then_inc(std_done, 1)
                act.wait_ge(tok_done, 1)
                act.copy(vst[:, :, 0:KVR], kc[:, :, 0:KVR]).then_inc(vh_done, 1)
                for t in range(ST):
                    at = slice(t * P, (t + 1) * P)
                    act.wait_ge(turned, t + 1)
                    act.copy(kh[:, at], ps[:, t % 2, 0:P])
                    act.copy(ikh[:, at], ps[:, t % 2, P:2 * P])
                    act.copy(qlh[:, :, at], ps[0:QC, t % 2, 2 * P:].rearrange("p (k n) -> p k n", k=2)).then_inc(hi_done, 1)

            @block.vector
            def _(dve):
                n = 0

                def step(ins):
                    nonlocal n
                    n += 1
                    ins.then_inc(dve_step, 1)
                    dve.wait_ge(dve_step, n)

                dve.wait_ge(lat_done, ST)
                dve.wait_ge(c_in, 48)
                step(dve.tensor_tensor(sq[:, :, :], lat[:, :, 0:QR + KVR], lat[:, :, 0:QR + KVR], ALU.mult))
                dve.tensor_reduce(ss[:, 0], sq[:, :, 0:QR], AX_X, ALU.add)
                step(dve.tensor_reduce(ss[:, 1], sq[:, :, QR:], AX_X, ALU.add))
                dve.tensor_scalar(ss[:, 0], ss[:, 0], 1.0 / QR, EPS, ALU.mult, ALU.add)
                dve.tensor_scalar(ss[:, 1], ss[:, 1], 1.0 / KVR, EPS, ALU.mult, ALU.add).then_inc(ss_done, 1)
                dve.wait_ge(std_done, 1)
                step(dve.reciprocal(rs[:, :, :], ss[:, :, :]))
                for t in range(ST):
                    dve.scalar_tensor_tensor(out=ql[:, t], in0=lat[:, t, 0:QR], scalar=rs[:, 0, t:t + 1], in1=qn[:, :],
                                             op0=ALU.mult, op1=ALU.mult)
                    dve.scalar_tensor_tensor(out=kc[:, t, 0:KVR], in0=lat[:, t, C_KV:C_KV + KVR],
                                             scalar=rs[:, 1, t:t + 1], in1=kvn[:, :], op0=ALU.mult, op1=ALU.mult)
                pe_pair = lat[:, :, C_PE:C_PE + ROPE].rearrange("p t (n e) -> p t n e", e=2)
                for j, (e, sc) in enumerate(((0, 0), (1, 1), (1, 0), (0, 1))):
                    ins = dve.tensor_tensor(rot[:, j], pe_pair[:, :, :, e], rope[:, :, sc, :], ALU.mult)
                step(ins)
                dve.tensor_tensor(kc[:, :, 64:96], rot[:, 0], rot[:, 1], ALU.subtract)
                dve.tensor_tensor(kc[:, :, 96:128], rot[:, 2], rot[:, 3], ALU.add)
                iw = lat[:, :, C_IW:C_IW + IH]
                dve.tensor_scalar(sg[:, :, :], iw, 0.0, 2.0, ALU.is_ge, ALU.mult)
                dve.tensor_scalar(aw[:, :, :], iw, IH ** -0.5 * ID ** -0.5, None, ALU.mult).then_inc(tok_done, 1)
                dve.wait_ge(tok_done, 1)
                step(dve.tensor_scalar(sg[:, :, :], sg[:, :, :], -1.0, None, ALU.add))
                dve.tensor_tensor(aw[:, :, :], aw[:, :, :], sg[:, :, :], ALU.mult)
                dve.wait_ge(vh_done, 1)
                dve.tensor_tensor(vst[:, :, KVR:], kc[:, :, 0:KVR], f32(vst[:, :, 0:KVR]), ALU.subtract)
                for t in range(ST):
                    at = slice(t * P, (t + 1) * P)
                    dve.wait_ge(hi_done, t + 1)
                    dve.tensor_tensor(kl[:, at], ps[:, t % 2, 0:P], f32(kh[:, at]), ALU.subtract)
                    dve.tensor_tensor(ikl[:, at], ps[:, t % 2, P:2 * P], f32(ikh[:, at]), ALU.subtract)
                    dve.tensor_tensor(qll[:, :, at], ps[0:QC, t % 2, 2 * P:].rearrange("p (k n) -> p k n", k=2),
                                      f32(qlh[:, :, at]), ALU.subtract).then_inc(lo_done[t % 2], 1)
        c.clear()


def index_scores(nc, ps, causal, xnh, xnl, wq_w, ikh, ikl, aw, sg, idx):
    with ExitStack() as st:
        c = Ctx(nc, st)
        w = c.sb("ix_w", [P, 2, DT, P])
        wh = c.sb("ix_wh", [P, 2, DT, P], F32R)
        wl = c.sb("ix_wl", [P, 2, DT, P], F32R)
        iqh = c.sb("ix_iqh", [P, 2, S], F32R)
        iql = c.sb("ix_iql", [P, 2, S], F32R)
        awc = c.sb("ix_awc", [P, 2, ST])
        sgc = c.sb("ix_sgc", [P, 2, ST])
        r = c.sb("ix_r", [P, 2, S])
        wh_done, wl_done, projected, iqh_done, iql_done, wc_done, scored = (
            c.sem("ix_" + n) for n in ("wh_done", "wl_done", "projected", "iqh_done", "iql_done", "wc_done", "scored"))
        raw_in = c.sems("ix_raw_in", 2)
        relu_done = c.sems("ix_relu_done", 2)
        added = c.sems("ix_added", 2)
        added_zero = c.sem("ix_added_zero")
        w_v = wq_w.rearrange("(k p) (j a n) -> j p a k n", p=P, a=2, n=ID)
        NP = IH // 2
        slots = [ps[:, 2 * k:2 * k + 2, :].rearrange("p b n -> p (b n)") for k in range(2)]
        ps_iq = ps[:, 6:8, :].rearrange("p b n -> p (b n)")

        def pairs(eng, body):
            with eng.Fori(0, NP - 1) as i:
                body(i, False)
            body(NP - 1, True)

        with nc.Block() as block:
            @block.sync
            def _(sp):
                with sp.Fori(0, NP) as i:
                    for a in range(2):
                        sp.wait_ge(wl_done, i * 2)
                        for k in range(DT):
                            sp.dma_start(w[:, a, k], w_v[i][:, a, k]).then_inc(raw_in[a], 16)

            @block.gpsimd
            def _(pool):
                with pool.Fori(0, NP) as i:
                    for a in range(2):
                        pool.wait_ge(wh_done, i * 2 + a + 1)
                        pool.tensor_tensor(wl[:, a], w[:, a], f32(wh[:, a]), ALU.subtract).then_inc(wl_done, 1)

            @block.tensor
            def _(pe):
                def project(n, a):
                    pe.wait_ge(wl_done, n + 1)
                    pe.wait_ge(iql_done, n)
                    for k in range(DT):
                        for h in range(2):
                            at = slice(h * HALF, (h + 1) * HALF)
                            ins = mm3(pe, ps_iq[:, at], (wh[:, a, k], wl[:, a, k]), (xnh[:, k, at], xnl[:, k, at]),
                                      k == 0, k == DT - 1)
                    ins.then_inc(projected, 1)

                def score(i, a):
                    pe.wait_ge(iql_done, i * 2 + a + 1)
                    for t in range(ST):
                        u = a * ST + t
                        pe.wait_ge(relu_done[u % 2], i * ST + u // 2)
                        at = slice(t * P, (t + 1) * P)
                        for j, (l, rr) in enumerate(((iqh, ikh), (iqh, ikl), (iql, ikh))):
                            for k0 in range(0, (t + 1) * P, HALF):
                                k1 = min(k0 + HALF, (t + 1) * P)
                                ins = pe.matmul(slots[u % 2][:, k0:k1], l[:, a, at], rr[:, k0:k1],
                                                start=j == 0, stop=j == 2, skip_group_check=True)
                        ins.then_inc(scored, 1)

                def body(i, last):
                    project(i * 2 + 1, 1)
                    score(i, 0)
                    if not last:
                        project(i * 2 + 2, 0)
                    score(i, 1)
                project(0, 0)
                pairs(pe, body)

            @block.scalar
            def _(act):
                def split_w(j, a):
                    act.wait_ge(raw_in[a], j * 64 + 64)
                    act.copy(wh[:, a], w[:, a]).then_inc(wh_done, 1)

                def split_iq(n, a):
                    act.wait_ge(projected, n + 1)
                    act.copy(iqh[:, a], ps_iq).then_inc(iqh_done, 1)

                def relus(i, a):
                    act.wait_ge(wc_done, i * 2 + a + 1)
                    for t in range(ST):
                        u = a * ST + t
                        act.wait_ge(scored, i * 2 * ST + u + 1)
                        act.wait_ge(added[u % 2], i * ST + u // 2)
                        W = (t + 1) * P
                        act.activation(r[:, u % 2, 0:W], slots[u % 2][:, 0:W], ACT.Relu,
                                       scale=awc[:, a, t:t + 1]).then_inc(relu_done[u % 2], 1)

                def body(i, last):
                    split_iq(i * 2 + 1, 1)
                    if not last:
                        split_w(i + 1, 0)
                    relus(i, 0)
                    if not last:
                        split_iq(i * 2 + 2, 0)
                        split_w(i + 1, 1)
                    relus(i, 1)
                split_w(0, 0)
                split_w(0, 1)
                split_iq(0, 0)
                pairs(act, body)

            @block.vector
            def _(dve):
                def split_iq(n, a):
                    dve.wait_ge(iqh_done, n + 1)
                    dve.tensor_tensor(iql[:, a], ps_iq, f32(iqh[:, a]), ALU.subtract).then_inc(iql_done, 1)

                def pick_w(i, a):
                    dve.tensor_copy(awc[:, a, :], aw[:, :, bass.ds(i * 2 + a, 1)].rearrange("p t o -> p (t o)"))
                    dve.tensor_copy(sgc[:, a, :], sg[:, :, bass.ds(i * 2 + a, 1)].rearrange("p t o -> p (t o)")).then_inc(
                        wc_done, 1)
                    dve.wait_ge(wc_done, i * 2 + a + 1)

                def adds(i, a):
                    for t in range(ST):
                        u = a * ST + t
                        dve.wait_ge(relu_done[u % 2], i * ST + u // 2 + 1)
                        W = (t + 1) * P
                        acc = idx[:, MASK_OFF[t]:MASK_OFF[t] + W]
                        dve.scalar_tensor_tensor(out=acc, in0=r[:, u % 2, 0:W], scalar=sgc[:, a, t:t + 1], in1=acc,
                                                 op0=ALU.mult, op1=ALU.add).then_inc(added[u % 2], 1)

                def body(i, last):
                    split_iq(i * 2 + 1, 1)
                    pick_w(i, 0)
                    adds(i, 0)
                    if not last:
                        split_iq(i * 2 + 2, 0)
                    pick_w(i, 1)
                    adds(i, 1)
                dve.memset(idx[:, :], 0.0).then_inc(added_zero, 1)
                dve.wait_ge(added_zero, 1)
                split_iq(0, 0)
                pairs(dve, body)
        c.clear()


def ffn(nc, tag, ps, xnh, xnl, x, F, w1_d, w3_d, w2_d, b1_d, b2_d, out_d=None, beside=None):
    gated = w3_d is not None
    NW = 2 if gated else 1
    NC = -(-F // P)
    size = [min(P, F - P * k) for k in range(NC)]
    LOOPS = (NC - 2) // 2
    with ExitStack() as st:
        c = Ctx(nc, st)
        w1 = c.sb(tag + "_w1", [P, 2, NW, DT, P])
        w1h = c.sb(tag + "_w1h", [P, 2, NW, DT, P], F32R)
        w1l = c.sb(tag + "_w1l", [P, 2, NW, DT, P], F32R)
        w2 = c.sb(tag + "_w2", [P, 2, D])
        w2h = c.sb(tag + "_w2h", [P, 2, D], F32R)
        w2l = c.sb(tag + "_w2l", [P, 2, D], F32R)
        g = c.sb(tag + "_g", [P, 2, HALF])
        g1 = c.sb(tag + "_g1", [P, 2, NW, HALF])
        gh = c.sb(tag + "_gh", [P, 2, HALF], F32R)
        gl = c.sb(tag + "_gl", [P, 2, HALF], F32R)
        y = c.sb(tag + "_y", [P, 4, D])
        ones = c.sb(tag + "_ones", [1, P])
        b2 = c.sb(tag + "_b2", [1, D])
        b1 = c.sb(tag + "_b1", [P, NC])
        b2_seen = c.sb(tag + "_b2_seen", [1, 1])
        names = ("b_in", "b_done", "seeded", "out_done", "x_done", "stored")
        b_in, b_done, seeded, out_done, x_done, stored = (c.sem(f"{tag}_{n}") for n in names)
        (w1_in, w2_in, w1h_done, w1l_done, w2h_done, w2l_done, hidden, act_done, g_done, gh_done, gl_done, used) = (
            c.sems(f"{tag}_{n}_", 2) for n in ("w1_in", "w2_in", "w1h_done", "w1l_done", "w2h_done", "w2l_done",
                                               "hidden", "act_done", "g_done", "gh_done", "gl_done", "used"))
        w1_v = [w.rearrange("(k p) n -> p k n", p=P) for w in ((w1_d, w3_d) if gated else (w1_d,))]
        uses = [(NC + 1) // 2, NC // 2]

        def ahead(j, s, by):
            return (j + (s + by) // 2, (s + by) % 2)

        def steps(eng, body):
            with eng.Fori(0, LOOPS) as i:
                for s in range(2):
                    body(i, s, (P, P, P))
            for k in range(2 * LOOPS, NC):
                body(k // 2, k % 2, [size[m] if m < NC else None for m in (k, k + 1, k + 2)])

        with nc.Block() as block:
            @block.sync
            def _(sp):
                if not gated:
                    sp.dma_start(b2[:, :], b2_d.rearrange("(o n) -> o n", o=1)).then_inc(b_in, 16)
                    sp.dma_start(b1[:, :], b1_d.rearrange("(k p) -> p k", p=P), allow_slow_non_contiguous=True).then_inc(b_in, 16)
                for half in range(2):
                    def body(j, s, sizes):
                        u, n = half * uses[s] + j, sizes[0]
                        at = bass.ds(j * 2 * P + s * P, n)
                        sp.wait_ge(w1l_done[s], u)
                        for m in range(NW):
                            sp.dma_start(w1[:, s, m, :, 0:n], w1_v[m][:, :, at]).then_inc(w1_in[s], 16)
                        sp.wait_ge(w2l_done[s], u)
                        sp.dma_start(w2[0:n, s], w2_d[at, :]).then_inc(w2_in[s], 16)
                    steps(sp, body)
                if out_d is not None:
                    for half in range(2):
                        sp.wait_ge(x_done, half + 1)
                        sp.dma_start(out_d.rearrange("(t p) n -> p t n", p=P)[:, 4 * half:4 * half + 4],
                                     x[:, 4 * half:4 * half + 4]).then_inc(stored, 16)
                    sp.wait_ge(stored, 32)

            @block.tensor
            def _(pe):
                for half in range(2):
                    tok = slice(half * HALF, (half + 1) * HALF)

                    def up(j, s, n):
                        u = half * uses[s] + j
                        pe.wait_ge(w1l_done[s], u + 1)
                        pe.wait_ge(act_done[s], u)
                        for m in range(NW):
                            for k in range(DT):
                                ins = mm3(pe, ps[0:n, 4 + NW * s + m, :], (w1h[:, s, m, k, 0:n], w1l[:, s, m, k, 0:n]),
                                          (xnh[:, k, tok], xnl[:, k, tok]), k == 0, k == DT - 1)
                        ins.then_inc(hidden[s], 1)

                    def down(j, s, n):
                        u = half * uses[s] + j
                        pe.wait_ge(w2l_done[s], u + 1)
                        pe.wait_ge(gl_done[s], u + 1)
                        for t in range(4):
                            at = slice(t * P, (t + 1) * P)
                            ins = mm3(pe, ps[:, t, :], (gh[0:n, s, at], gl[0:n, s, at]), (w2h[0:n, s], w2l[0:n, s]),
                                      False, True)
                        ins.then_inc(used[s], 1)

                    def body(j, s, sizes):
                        if sizes[1] is not None:
                            up(*ahead(j, s, 1), sizes[1])
                        down(j, s, sizes[0])

                    up(0, 0, size[0])
                    pe.wait_ge(b_done, 2)
                    pe.wait_ge(out_done, half)
                    for t in range(4):
                        pe.matmul(ps[:, t, :], ones[:, :], b2[:, :], start=True, stop=False, skip_group_check=True)
                    steps(pe, body)

            @block.scalar
            def _(act):
                for half in range(2):
                    def split_w1(j, s, n):
                        u = half * uses[s] + j
                        act.wait_ge(w1_in[s], (u + 1) * 16 * NW)
                        act.wait_ge(hidden[s], u)
                        act.copy(w1h[:, s, :, :, 0:n], w1[:, s, :, :, 0:n]).then_inc(w1h_done[s], 1)

                    def split_w2(j, s, n):
                        u = half * uses[s] + j
                        act.wait_ge(w2_in[s], (u + 1) * 16)
                        act.wait_ge(used[s], u)
                        act.copy(w2h[0:n, s], w2[0:n, s]).then_inc(w2h_done[s], 1)

                    def activate(j, s, n):
                        u = half * uses[s] + j
                        act.wait_ge(hidden[s], u + 1)
                        if gated:
                            act.wait_ge(g_done[s], u)
                            act.activation(g1[0:n, s, 0], ps[0:n, 4 + 2 * s, :], ACT.Silu)
                            act.copy(g1[0:n, s, 1], ps[0:n, 5 + 2 * s, :]).then_inc(act_done[s], 1)
                            act.wait_ge(g_done[s], u + 1)
                        else:
                            act.wait_ge(gl_done[s], u)
                            bias = b1[0:n, bass.ds(j * 2 + s, 1)]
                            act.activation(g[0:n, s], ps[0:n, 4 + s, :], ACT.Gelu_apprx_tanh, bias=bias).then_inc(
                                act_done[s], 1)
                            act.wait_ge(act_done[s], u + 1)
                        act.wait_ge(used[s], u)
                        act.copy(gh[0:n, s], g[0:n, s]).then_inc(gh_done[s], 1)

                    def body(j, s, sizes):
                        if sizes[2] is not None:
                            split_w1(*ahead(j, s, 2), sizes[2])
                        if sizes[1] is not None:
                            split_w2(*ahead(j, s, 1), sizes[1])
                            activate(*ahead(j, s, 1), sizes[1])

                    if half == 0 and not gated:
                        act.wait_ge(b_in, 32)
                    split_w1(0, 0, P)
                    split_w1(0, 1, P)
                    split_w2(0, 0, P)
                    activate(0, 0, P)
                    steps(act, body)
                    for s in range(2):
                        act.wait_ge(used[s], (half + 1) * uses[s])
                    act.wait_ge(x_done, half)
                    act.copy(y[:, :, :], ps[:, 0:4, :]).then_inc(out_done, 1)

            @block.gpsimd
            def _(pool):
                pool.memset(ones[:, :], 1.0).then_inc(b_done, 1)
                if gated:
                    pool.memset(b2[:, :], 0.0).then_inc(b_done, 1)
                else:
                    pool.wait_ge(b_in, 32)
                    pool.memset(b2_seen[:, :], 0.0).then_inc(b_done, 1)
                for half in range(2):
                    def split_w1(j, s, n):
                        u = half * uses[s] + j
                        pool.wait_ge(w1h_done[s], u + 1)
                        for m in range(NW):
                            ins = pool.tensor_tensor(w1l[:, s, m, :, 0:n], w1[:, s, m, :, 0:n],
                                                     f32(w1h[:, s, m, :, 0:n]), ALU.subtract)
                        ins.then_inc(w1l_done[s], 1)

                    def split_w2(j, s, n):
                        u = half * uses[s] + j
                        pool.wait_ge(w2h_done[s], u + 1)
                        pool.tensor_tensor(w2l[0:n, s], w2[0:n, s], f32(w2h[0:n, s]), ALU.subtract).then_inc(
                            w2l_done[s], 1)

                    def split_g(j, s, n):
                        u = half * uses[s] + j
                        if gated:
                            pool.wait_ge(act_done[s], u + 1)
                            pool.wait_ge(gl_done[s], u)
                            pool.tensor_tensor(g[0:n, s], g1[0:n, s, 0], g1[0:n, s, 1], ALU.mult).then_inc(g_done[s], 1)
                        pool.wait_ge(gh_done[s], u + 1)
                        pool.tensor_tensor(gl[0:n, s], g[0:n, s], f32(gh[0:n, s]), ALU.subtract).then_inc(gl_done[s], 1)

                    def body(j, s, sizes):
                        if sizes[2] is not None:
                            split_w1(*ahead(j, s, 2), sizes[2])
                        if sizes[1] is not None:
                            split_w2(*ahead(j, s, 1), sizes[1])
                            split_g(*ahead(j, s, 1), sizes[1])

                    split_w1(0, 0, P)
                    split_w1(0, 1, P)
                    split_w2(0, 0, P)
                    split_g(0, 0, P)
                    steps(pool, body)
                    pool.wait_ge(out_done, half + 1)
                    mine = x[:, 4 * half:4 * half + 4]
                    pool.tensor_tensor(mine, mine, y[:, :, :], ALU.add).then_inc(x_done, 1)

            if beside is not None:
                @block.vector
                def _(dve):
                    beside(dve)
        c.clear()


def attention(nc, tag, ps, IT, HP, passes, mask_of, scale, vst, qwork, ctx_d, peel):
    NU = HP * ST
    AHEAD = 7
    NT = 3
    CPH = 12
    layer0 = qwork["layer0"]
    with ExitStack() as st:
        c = Ctx(nc, st)
        sm = [c.sb(f"{tag}_sm{k}", [P, (S, HALF)[k]]) for k in range(2)]
        p = [c.sb(f"{tag}_p{k}", [P, 2, (S, HALF)[k]]) for k in range(2)]
        nmax = c.sb(tag + "_nmax", [P, 4])
        rsum = c.sb(tag + "_rsum", [P, 4])
        rinv = c.sb(tag + "_rinv", [P, 4])
        pth = [c.sb(f"{tag}_pth{g}", [P, 4 * g + 4, HALF], F32R) for g in range(2)]
        ptl = [c.sb(f"{tag}_ptl{g}", [P, 4 * g + 4, HALF], F32R) for g in range(2)]
        ctxst = c.sb(tag + "_ctxst", [P, S])
        (scored, max_done, exp_done, inv_done, norm_done, turned, hi_done, ctx_done) = (
            c.sem(f"{tag}_{n}") for n in ("scored", "max_done", "exp_done", "inv_done", "norm_done", "turned",
                                          "hi_done", "ctx_done"))
        passed, stored = c.sem(tag + "_passed"), c.sem(tag + "_sp_passed")
        lo_done = c.sems(tag + "_lo_done", NT)
        pv_done, ctx_out = c.sem(tag + "_pv_done"), c.sem(tag + "_ctx_out")
        slots = [ps[:, 0:2, :].rearrange("p b n -> p (b n)"), ps[:, 2, :]]
        bank_t = (3, 4, 5)
        banks_c = (6,) if layer0 else (6, 7)
        results = [ps[:, b, 0:PAIR] for b in banks_c]
        parts = [(1, 4), (2, 2), (5, 6), (6, 0)]
        sems = dict(scored=scored, ctx_done=ctx_done, pv_done=pv_done)

        def unit(v):
            a, r = divmod(v, ST)
            t = 4 + r // 2 if r % 2 == 0 else 3 - r // 2
            return a, t, r % 2, (t + 1) * P

        def chunks_of(v):
            r = v % ST
            t = unit(v % NU)[1]
            if r % 2 == 0:
                return [(3 * (r // 2), 0, 4), (3 * (r // 2) + 1, 4, t - 3)]
            return [(3 * (r // 2) + 2, 0, t + 1)]

        def run(eng, step):
            def body(i, left):
                for u in range(NU):
                    step(i, u, left)
            for u in range(-AHEAD, 0):
                step(0, u, IT)
            with eng.Fori(0, IT - peel) as i:
                body(i, peel)
            for left in reversed(range(peel)):
                body(IT - 1 - left, left)

        def there(v, left):
            return v >= 0 and (v < NU or left > 0)

        q = qwork["make"](c, sems)

        with nc.Block() as block:
            @block.tensor
            def _(pe):
                def scores(i, v):
                    a, t, kind, w = unit(v % NU)
                    q["ready"](pe, i, v)
                    if v >= 2:
                        pe.wait_ge(max_done, i * NU + v - 1)
                    at = slice(t * P, (t + 1) * P)
                    lr = passes(i, v // NU, a)
                    for j, (l, r) in enumerate(lr):
                        for k0 in range(0, w, HALF):
                            k1 = min(k0 + HALF, w)
                            ins = pe.matmul(slots[kind][:, k0:k1], l(at), r(k0, k1), start=j == 0,
                                            stop=j == len(lr) - 1, skip_group_check=True)
                    ins.then_inc(scored, 1)

                def turn(i, v):
                    _, t, kind, w = unit(v % NU)
                    pe.wait_ge(norm_done, i * NU + v + 1)
                    for n, j0, m in chunks_of(v):
                        if v >= 2:
                            pe.wait_ge(lo_done[n % NT], (i * HP + v // ST) * (CPH // NT) + n // NT)
                        for k in range(m):
                            ins = pe.transpose(ps[:, bank_t[n % NT], k * P:(k + 1) * P],
                                               p[kind][:, v // 2 % 2, (j0 + k) * P:(j0 + k + 1) * P],
                                               qwork["ident"][:, :])
                        ins.then_inc(turned, 1)

                def weigh(i, a, k, t):
                    g = t // 4
                    last = max(2 * (t % 4) + 2, 0) if g else 2 * (3 - t) + 1
                    for n, _, _ in chunks_of(last):
                        pe.wait_ge(lo_done[n % NT], (i * HP + a) * (CPH // NT) + n // NT + 1)
                    pe.wait_ge(ctx_done, (i * HP + a) * 4 + k + 1)
                    for j in range(t + 2):
                        n0 = PAIR // 2 if j == t + 1 else 0
                        c0 = t % 4 * P
                        for h, pt in enumerate((pth[g], ptl[g])):
                            ins = pe.matmul(results[k % len(banks_c)][:, n0:PAIR], vst(j), pt[:, j, c0 + n0:c0 + PAIR],
                                            start=j == 0 and h == 0, stop=j == t + 1 and h == 1,
                                            skip_group_check=True)
                    ins.then_inc(pv_done, 1)

                def step(i, u, left):
                    if there(u + 7, left):
                        scores(i, u + 7)
                    if there(u + 3, left):
                        turn(i, u + 3)
                    q["pe"](pe, i, u, left)
                    for k, (s, t) in enumerate(parts):
                        if u >= 0 and u % ST == s:
                            q["v_ready"](pe, i, u // ST, k)
                            weigh(i, u // ST, k, t)

                pe.sem_inc(ctx_done, len(banks_c))
                q["pe_first"](pe)
                run(pe, step)

            @block.vector
            def _(dve):
                def maximum(i, v):
                    a, t, kind, w = unit(v % NU)
                    pause(dve, scored, i * NU + v + 1, passed)
                    dve.tensor_tensor_reduce(out=sm[kind][:, 0:w], in0=slots[kind][:, 0:w], in1=mask_of(t),
                                             scale=-scale, scalar=3.0e38, op0=ALU.add, op1=ALU.min,
                                             accum_out=nmax[:, v % 4:v % 4 + 1]).then_inc(max_done, 1)

                def inverse(i, v):
                    k = v % 4
                    dve.wait_ge(exp_done, i * NU + v + 1)
                    dve.reciprocal(rinv[:, k:k + 1], rsum[:, k:k + 1]).then_inc(inv_done, 1)

                def low(i, v):
                    _, t, kind, w = unit(v % NU)
                    g = t // 4
                    at = slice((t % 4) * P, (t % 4 + 1) * P)
                    for n, j0, m in chunks_of(v):
                        dve.wait_ge(hi_done, (i * HP + v // ST) * CPH + n + 1)
                        dve.tensor_tensor(ptl[g][:, j0:j0 + m, at], bank4(ps, bank_t[n % NT])[:, 0:m],
                                          f32(pth[g][:, j0:j0 + m, at]), ALU.subtract).then_inc(lo_done[n % NT], 1)

                def step(i, u, left):
                    if there(u + 5, left):
                        inverse(i, u + 5)
                    q["dve"](dve, i, u, left)
                    for k, (s, t) in enumerate(parts):
                        if layer0 and u >= 0 and u % ST == s + 1:
                            q["dve_ctx"](dve, i, u // ST, k, results[k % len(banks_c)], ctxst[:, t * P:t * P + PAIR], ctx_out)
                    if there(u + 7, left):
                        maximum(i, u + 7)
                    if there(u + 2, left):
                        low(i, u + 2)

                q["dve_first"](dve)
                run(dve, step)

            @block.scalar
            def _(act):
                def exponential(i, v):
                    a, t, kind, w = unit(v % NU)
                    act.wait_ge(max_done, i * NU + v + 1)
                    act.activation(p[kind][:, v // 2 % 2, 0:w], sm[kind][:, 0:w], ACT.Exp,
                                   bias=nmax[:, v % 4:v % 4 + 1], scale=-1.0,
                                   accum_out=rsum[:, v % 4:v % 4 + 1]).then_inc(exp_done, 1)

                def high(i, v):
                    _, t, kind, w = unit(v % NU)
                    g = t // 4
                    at = slice((t % 4) * P, (t % 4 + 1) * P)
                    for n, j0, m in chunks_of(v):
                        act.wait_ge(turned, (i * HP + v // ST) * CPH + n + 1)
                        act.copy(pth[g][:, j0:j0 + m, at], bank4(ps, bank_t[n % NT])[:, 0:m]).then_inc(hi_done, 1)

                def step(i, u, left):
                    if there(u + 6, left):
                        exponential(i, u + 6)
                    for k, (s, t) in enumerate(parts):
                        if u >= 0 and u % ST == s + 1:
                            q["act_ctx"](act, i, u // ST, k, results[k % len(banks_c)], ctxst[:, t * P:t * P + PAIR], ctx_out)
                    if there(u + 3, left):
                        high(i, u + 3)
                    q["act"](act, i, u, left)

                q["act_first"](act)
                run(act, step)

            @block.gpsimd
            def _(pool):
                def normalise(i, v):
                    a, t, kind, w = unit(v % NU)
                    pause(pool, inv_done, i * NU + v + 1, passed)
                    mine = p[kind][:, v // 2 % 2, 0:w]
                    pool.tensor_scalar(mine, mine, rinv[:, v % 4:v % 4 + 1], 1.0, ALU.mult, ALU.mult).then_inc(
                        norm_done, 1)

                def step(i, u, left):
                    if there(u + 5, left):
                        normalise(i, u + 5)
                    q["pool"](pool, i, u, left)

                q["pool_first"](pool)
                run(pool, step)

            @block.sync
            def _(sp):
                sp.sem_inc(ctx_out, 1)
                q["sp_first"](sp)

                def body(i, left):
                    q["sp"](sp, i, left)
                    pause(sp, ctx_done, (i + 1) * 4 * HP + len(banks_c), stored)
                    sp.dma_start(ctx_d[i], ctxst[:, :]).then_inc(ctx_out, 16)
                with sp.Fori(0, IT - peel) as i:
                    body(i, peel)
                for left in reversed(range(peel)):
                    body(IT - 1 - left, left)
                sp.wait_ge(ctx_out, 16 * IT + 1)
        c.clear()


def latent_queries(nc, ps, ident, xq, wabs_d, cos_d, sin_d, tables):
    qlh, qll = xq
    cosT, sinT = tables
    pieces = [(0, "sw", 0, 0), (1, "sw", 0, 1), (2, "m", 0, 0), (4, "m", 0, 1), (8, "m", 1, 0), (10, "m", 1, 1)]
    NPC = len(pieces)
    W_STEP = 12
    bank_q = 7
    q = {"layer0": True, "ident": ident}

    def make(c, sems):
        wraw = c.sb("lq_wraw", [QC, 2, 3, P])
        wh = c.sb("lq_wh", [QC, 2, 3, P], F32R)
        wl = c.sb("lq_wl", [QC, 2, 3, P], F32R)
        t1 = c.sb("lq_t1", [P, 2, HALF])
        t2 = c.sb("lq_t2", [P, 2, S])
        qh = c.sb("lq_qh", [P, 2, S], F32R)
        ql = c.sb("lq_ql", [P, 2, S], F32R)
        tmp = c.sb("lq_tmp", [KVR, 2, PAIR])
        raw_in, tab_in, wh_done, wl_done, q_mm, q_evac, add_done, qh_done, q_lo_done, tmp_done = (
            c.sem("lq_" + n) for n in ("raw_in", "tab_in", "wh_done", "wl_done", "q_mm", "q_evac", "add_done",
                                       "qh_done", "q_lo_done", "tmp_done"))
        scored, ctx_done, pv_done = sems["scored"], sems["ctx_done"], sems["pv_done"]
        q["bufs"] = (qh, ql)

        def ready(pe, i, v):
            if v % ST == 0:
                pe.wait_ge(q_lo_done, i * 4 + 2 * (v // ST) + 2)

        def piece(pair, k):
            return pair * NPC + k, pair * 4 + k - 2

        def of_step(u, left):
            return [k for k, (s, _, _, _) in enumerate(pieces) if s == u and left > 0]

        def pe_piece(pe, pair, k):
            _, kind, a, g = pieces[k]
            K, M = piece(pair, k)
            pe.wait_ge(wl_done, pair + 1)
            pe.wait_ge(q_evac, K)
            b = a if kind == "m" else 2
            at = slice(g * HALF, (g + 1) * HALF)
            for h in range(2):
                ins = mm3(pe, ps[:, bank_q, :], (wh[:, h, b], wl[:, h, b]), (qlh[:, h, at], qll[:, h, at]),
                          h == 0, h == 1)
            ins.then_inc(q_mm, 1)

        def dve_piece(dve, pair, k, first=False):
            _, kind, a, g = pieces[k]
            K, M = piece(pair, k)
            dve.wait_ge(q_mm, K + 1)
            at = slice(g * HALF, (g + 1) * HALF)
            if kind == "sw":
                if not first:
                    dve.wait_ge(add_done, pair * 4)
                for h in range(2):
                    rows = slice(64 * h, 64 * h + 64)
                    ins = dve.tensor_tensor(t2[64:P, h, at], ps[rows, bank_q, :], sinT[rows, at], ALU.mult)
            else:
                if not first or k >= 4:
                    dve.wait_ge(q_lo_done, M - 1)
                ins = dve.tensor_tensor(t1[:, g], ps[:, bank_q, :], cosT[:, at], ALU.mult)
            ins.then_inc(q_evac, 1)

        def pool_add(pool, pair, k):
            _, kind, a, g = pieces[k]
            pool.wait_ge(q_evac, piece(pair, k)[0] + 1)
            pool.tensor_tensor(t1[:, g], t1[:, g], t2[:, a, g * HALF:(g + 1) * HALF], ALU.add).then_inc(add_done, 1)

        def act_high(act, pair, k, first=False):
            _, kind, a, g = pieces[k]
            act.wait_ge(add_done, piece(pair, k)[1] + 1)
            if not first:
                act.wait_ge(scored, (pair - 1) * 2 * ST + (a + 1) * ST)
            act.copy(qh[:, a, g * HALF:(g + 1) * HALF], t1[:, g]).then_inc(qh_done, 1)

        def pool_low(pool, pair, k):
            _, kind, a, g = pieces[k]
            pool.wait_ge(qh_done, piece(pair, k)[1] + 1)
            at = slice(g * HALF, (g + 1) * HALF)
            pool.tensor_tensor(ql[:, a, at], t1[:, g], f32(qh[:, a, at]), ALU.subtract).then_inc(q_lo_done, 1)

        def act_weights(act, pair, first=False):
            act.wait_ge(raw_in, pair * 16 + 16)
            if not first:
                act.wait_ge(q_mm, pair * NPC)
            act.copy(wh[:, :, :, :], wraw[:, :, :, :]).then_inc(wh_done, 1)

        def pool_weights(pool, pair):
            pool.wait_ge(wh_done, pair + 1)
            pool.tensor_tensor(wl[:, :, :, :], wraw[:, :, :, :], f32(wh[:, :, :, :]), ALU.subtract).then_inc(wl_done, 1)

        def load_weights(sp, pair):
            sp.dma_start(wraw[:, :, :, :].rearrange("p c b n -> p (c b n)"), wabs_d[pair]).then_inc(raw_in, 16)

        def pe_first(pe):
            for k in range(NPC):
                if k:
                    pe_piece(pe, 0, k)
                else:
                    pe.wait_ge(wl_done, 1)
                    for h in range(2):
                        ins = mm3(pe, ps[:, bank_q, :], (wh[:, h, 2], wl[:, h, 2]), (qlh[:, h, 0:HALF], qll[:, h, 0:HALF]),
                                  h == 0, h == 1)
                    ins.then_inc(q_mm, 1)

        def dve_first(dve):
            dve.memset(t2[0:64, :, :], 0.0)
            dve.wait_ge(tab_in, 32)
            for k in range(NPC):
                dve_piece(dve, 0, k, first=True)

        def act_first(act):
            act_weights(act, 0, first=True)
            for k in range(2, NPC):
                act_high(act, 0, k, first=True)
            act_weights(act, 1)

        def pool_first(pool):
            pool_weights(pool, 0)
            for k in range(2, NPC):
                pool_add(pool, 0, k)
                pool_low(pool, 0, k)
            pool_weights(pool, 1)

        def sp_first(sp):
            load_weights(sp, 0)
            sp.dma_start(cosT[:, :], cos_d).then_inc(tab_in, 16)
            sp.dma_start(sinT[:, :], sin_d).then_inc(tab_in, 16)
            sp.wait_ge(wl_done, 1)
            load_weights(sp, 1)

        def pe_hook(pe, i, u, left):
            for k in of_step(u, left):
                pe_piece(pe, i + 1, k)

        def dve_hook(dve, i, u, left):
            for k in of_step(u - 1, left):
                dve_piece(dve, i + 1, k)

        def act_hook(act, i, u, left):
            for k in of_step(u - 2, left):
                if k >= 2:
                    act_high(act, i + 1, k)
            if u == W_STEP and left > 1:
                act_weights(act, i + 2)

        def pool_hook(pool, i, u, left):
            for k in of_step(u - 3, left):
                if k >= 2:
                    pool_low(pool, i + 1, k)
            for k in of_step(u - 1, left):
                if k >= 2:
                    pool_add(pool, i + 1, k)
            if u == W_STEP + 1 and left > 1:
                pool_weights(pool, i + 2)

        def sp_hook(sp, i, left):
            if left > 1:
                sp.wait_ge(wl_done, i + 2)
                load_weights(sp, i + 2)

        def act_ctx(act, i, a, k, result, out, ctx_out):
            act.wait_ge(pv_done, (i * 2 + a) * 4 + k + 1)
            act.copy(tmp[:, k % 2], result[KVR:2 * KVR, :]).then_inc(tmp_done, 1)

        def dve_ctx(dve, i, a, k, result, out, ctx_out):
            dve.wait_ge(tmp_done, (i * 2 + a) * 4 + k + 1)
            if a == 0 and k == 0:
                dve.wait_ge(ctx_out, i * 16 + 1)
            dve.tensor_tensor(out[64 * a:64 * a + 64, :], result[0:KVR, :], tmp[:, k % 2], ALU.add).then_inc(ctx_done, 1)

        q.update(ready=ready, pe=pe_hook, dve=dve_hook, act=act_hook, pool=pool_hook, sp=sp_hook, pe_first=pe_first,
                 dve_first=dve_first, act_first=act_first, pool_first=pool_first, sp_first=sp_first, act_ctx=act_ctx,
                 dve_ctx=dve_ctx, v_ready=lambda *_: None)
        return q

    q["make"] = make
    return q


def stacked_queries(nc, ps, ident, vs_all, vg, qd, kvd):
    q = {"layer0": False, "ident": ident}
    q_v = qd.rearrange("l (i a p) t -> l i a p t", a=REP1, p=HD1)
    k_v = kvd.rearrange("l (g e p) t -> l e p g t", e=2, p=HD1)

    def make(c, sems):
        qst = c.sb("sq_qst", [P, REP1, S], F32R)
        kst = c.sb("sq_kst", [P, G1, S], F32R)
        zeroed, k_in, vg_done = c.sem("sq_zeroed"), c.sem("sq_k_in"), c.sem("sq_vg_done")
        q_in = c.sems("sq_q_in", REP1)
        scored, ctx_done, pv_done = sems["scored"], sems["ctx_done"], sems["pv_done"]
        q["bufs"] = (qst, kst)

        def load_q(sp, i, a):
            for b in range(4):
                sp.dma_start(f32(qst[b * HD1:(b + 1) * HD1, a]), q_v[b // 2][i][a]).then_inc(q_in[a], 16)

        def ready(pe, i, v):
            if v % ST == 0:
                a = (v // ST) % REP1
                pe.wait_ge(q_in[a], (i + v // (REP1 * ST)) * 64 + 64)

        def sp_first(sp):
            for a in range(REP1):
                load_q(sp, 0, a)
            for b in range(4):
                sp.dma_start(f32(kst[b * HD1:(b + 1) * HD1, :, :]), k_v[b % 2][0]).then_inc(k_in, 16)

        def sp_hook(sp, i, left):
            if left:
                for a in range(REP1):
                    sp.wait_ge(scored, i * REP1 * ST + (a + 1) * ST)
                    load_q(sp, i + 1, a)

        def dve_first(dve):
            dve.memset(f32(qst[64:P, :, :]), 0.0).then_inc(zeroed, 1)
            dve.memset(f32(kst[64:P, :, :]), 0.0).then_inc(zeroed, 1)

        def pe_first(pe):
            pe.wait_ge(zeroed, 2)
            pe.wait_ge(k_in, 64)

        def copy_values(act, i, first=False):
            if not first:
                act.wait_ge(pv_done, i * REP1 * 4)
            src = vs_all[:, :, bass.ds(i, 1), :].broadcast_to([P, ST, REP1, 2 * HD1])
            act.copy(vg[:, :, :, :], src).then_inc(vg_done, 1)

        def act_first(act):
            copy_values(act, 0, first=True)

        def act_hook(act, i, u, left):
            if u == REP1 * ST - 1 and left:
                copy_values(act, i + 1)

        def v_ready(pe, i, a, k):
            if a == 0 and k == 0:
                pe.wait_ge(vg_done, i + 1)

        def act_ctx(act, i, a, k, result, out, ctx_out):
            act.wait_ge(pv_done, (i * REP1 + a) * 4 + k + 1)
            if a == 0 and k == 0:
                act.wait_ge(ctx_out, i * 16 + 1)
            rows = slice(32 * a, 32 * a + 32)
            act.copy(out[rows, :], result[rows, :]).then_inc(ctx_done, 1)

        def none(*_):
            pass

        q.update(ready=ready, pe=none, dve=none, act=act_hook, pool=none, sp=sp_hook, pe_first=pe_first,
                 dve_first=dve_first, act_first=act_first, pool_first=none, sp_first=sp_first, act_ctx=act_ctx,
                 v_ready=v_ready)
        return q

    q["make"] = make
    return q


def project_out(nc, tag, ps, x, NK, ctx_d, load_w, w_dmas, bias_d):
    with ExitStack() as st:
        c = Ctx(nc, st)
        cr = c.sb(tag + "_cr", [P, 2, HALF])
        ch = c.sb(tag + "_ch", [P, 2, HALF], F32R)
        cl = c.sb(tag + "_cl", [P, 2, HALF], F32R)
        wr = c.sb(tag + "_wr", [P, 2, D])
        wh = c.sb(tag + "_wh", [P, 2, D], F32R)
        wl = c.sb(tag + "_wl", [P, 2, D], F32R)
        ones = c.sb(tag + "_ones", [1, P])
        b = c.sb(tag + "_b", [1, D])
        b_in, b_done, summed, x_done = (c.sem(f"{tag}_{n}") for n in ("b_in", "b_done", "summed", "x_done"))
        raw_in, hi_done, lo_done, used = (c.sems(f"{tag}_{n}_", 2) for n in ("raw_in", "hi_done", "lo_done", "used"))
        NJ = NK // 2

        def tiles(eng, half, body):
            with eng.Fori(0, NJ) as i:
                for s in range(2):
                    body(i * 2 + s, s, i + half * NJ)

        with nc.Block() as block:
            @block.sync
            def _(sp):
                if bias_d is not None:
                    sp.dma_start(b[:, :], bias_d.rearrange("(o n) -> o n", o=1)).then_inc(b_in, 16)
                for half in range(2):
                    def body(k, s, u):
                        sp.wait_ge(lo_done[s], u)
                        sp.dma_start(cr[:, s], ctx_d[k][:, half * HALF:(half + 1) * HALF]).then_inc(raw_in[s], 16)
                        load_w(sp, k, wr[:, s], raw_in[s])
                    tiles(sp, half, body)

            @block.scalar
            def _(act):
                for half in range(2):
                    def body(k, s, u):
                        act.wait_ge(raw_in[s], (u + 1) * 16 * (1 + w_dmas))
                        act.wait_ge(used[s], u)
                        act.copy(ch[:, s], cr[:, s])
                        act.copy(wh[:, s], wr[:, s]).then_inc(hi_done[s], 1)
                    tiles(act, half, body)

            @block.gpsimd
            def _(pool):
                pool.memset(ones[:, :], 1.0).then_inc(b_done, 1)
                if bias_d is None:
                    pool.memset(b[:, :], 0.0).then_inc(b_done, 1)
                for half in range(2):
                    def body(k, s, u):
                        pool.wait_ge(hi_done[s], u + 1)
                        pool.tensor_tensor(cl[:, s], cr[:, s], f32(ch[:, s]), ALU.subtract)
                        pool.tensor_tensor(wl[:, s], wr[:, s], f32(wh[:, s]), ALU.subtract).then_inc(lo_done[s], 1)
                    tiles(pool, half, body)

            @block.tensor
            def _(pe):
                pe.wait_ge(b_done, 1 if bias_d is not None else 2)
                if bias_d is not None:
                    pe.wait_ge(b_in, 16)
                for half in range(2):
                    for t in range(4):
                        pe.matmul(ps[:, 4 * half + t, :], ones[:, :], b[:, :], start=True, stop=False,
                                  skip_group_check=True)

                    def body(k, s, u):
                        pe.wait_ge(lo_done[s], u + 1)
                        for t in range(4):
                            at = slice(t * P, (t + 1) * P)
                            ins = mm3(pe, ps[:, 4 * half + t, :], (ch[:, s, at], cl[:, s, at]), (wh[:, s], wl[:, s]),
                                      False, True)
                        ins.then_inc(used[s], 1)
                    tiles(pe, half, body)

            @block.vector
            def _(dve):
                for half in range(2):
                    for s in range(2):
                        dve.wait_ge(used[s], (half + 1) * NJ)
                    mine = x[:, 4 * half:4 * half + 4]
                    dve.tensor_tensor(mine, ps[:, 4 * half:4 * half + 4, :], mine, ALU.add).then_inc(x_done, 1)
        c.clear()


def layer1_qkv(nc, ps, xnh, xnl, wq, wkv, qd, kvd, vs_all):
    NQ, NKV = D // P, 2 * G1 * HD1 // P
    with ExitStack() as st:
        c = Ctx(nc, st)
        NW = D + 2 * G1 * HD1
        w = c.sb("qk_w", [P, DT, NW])
        wh = c.sb("qk_wh", [P, DT, NW], F32R)
        wl = c.sb("qk_wl", [P, DT, NW], F32R)
        oh = c.sb("qk_oh", [P, NQ + NKV, S], F32R)
        ol = c.sb("qk_ol", [P, NQ + NKV, S], F32R)
        w_in, wh_done, wl_done, done, hi_done, lo_done, stored = (
            c.sem("qk_" + n) for n in ("w_in", "wh_done", "wl_done", "done", "hi_done", "lo_done", "stored"))
        tasks = [("T", m, h) for m in range(NQ + NKV) for h in range(2)] + [("V", t, 0) for t in range(ST)]
        with nc.Block() as block:
            @block.sync
            def _(sp):
                sp.dma_start(w[:, :, 0:D], wq.rearrange("(k p) n -> p k n", p=P)).then_inc(w_in, 16)
                sp.dma_start(w[:, :, D:], wkv.rearrange("(k p) n -> p k n", p=P)).then_inc(w_in, 16)
                for m in range(NQ + NKV):
                    sp.wait_ge(lo_done, 2 * m + 2)
                    for l, o in enumerate((oh, ol)):
                        dst = qd[l][m * P:(m + 1) * P, :] if m < NQ else kvd[l][(m - NQ) * P:(m - NQ + 1) * P, :]
                        sp.dma_start(dst, f32(o[:, m])).then_inc(stored, 16)
                sp.wait_ge(stored, 32 * (NQ + NKV))

            @block.gpsimd
            def _(pool):
                for m in range(0, NQ + NKV, 2):
                    pool.wait_ge(wh_done, m + 2)
                    at = slice((m + 1) * P, (m + 2) * P)
                    pool.tensor_tensor(wl[:, :, at], w[:, :, at], f32(wh[:, :, at]), ALU.subtract).then_inc(wl_done, 1)

            @block.scalar
            def _(act):
                act.wait_ge(w_in, 32)
                for m in range(NQ + NKV):
                    at = slice(m * P, (m + 1) * P)
                    act.copy(wh[:, :, at], w[:, :, at]).then_inc(wh_done, 1)
                for n, (kind, m, h) in enumerate(tasks):
                    act.wait_ge(done, n + 1)
                    if kind == "T":
                        act.copy(oh[:, m, h * HALF:(h + 1) * HALF], ps[:, n % 8, :]).then_inc(hi_done, 1)
                    else:
                        v = ps[:, n % 8, 0:2 * G1 * HD1].rearrange("p (g e n) -> p g e n", e=2, n=HD1)[:, :, 1, :]
                        act.copy(vs_all[:, m, :, 0:HD1], v).then_inc(hi_done, 1)

            @block.vector
            def _(dve):
                for m in range(0, NQ + NKV, 2):
                    dve.wait_ge(wh_done, m + 1)
                    at = slice(m * P, (m + 1) * P)
                    dve.tensor_tensor(wl[:, :, at], w[:, :, at], f32(wh[:, :, at]), ALU.subtract).then_inc(wl_done, 1)
                for n, (kind, m, h) in enumerate(tasks):
                    dve.wait_ge(hi_done, n + 1)
                    if kind == "T":
                        at = slice(h * HALF, (h + 1) * HALF)
                        dve.tensor_tensor(ol[:, m, at], ps[:, n % 8, :], f32(oh[:, m, at]), ALU.subtract).then_inc(lo_done, 1)
                    else:
                        v = ps[:, n % 8, 0:2 * G1 * HD1].rearrange("p (g e n) -> p g e n", e=2, n=HD1)[:, :, 1, :]
                        dve.tensor_tensor(vs_all[:, m, :, HD1:], v, f32(vs_all[:, m, :, 0:HD1]), ALU.subtract).then_inc(
                            lo_done, 1)

            @block.tensor
            def _(pe):
                pe.wait_ge(wl_done, NQ + NKV)
                for n, (kind, m, h) in enumerate(tasks):
                    if n >= 8:
                        pe.wait_ge(lo_done, n - 7)
                    for k in range(DT):
                        if kind == "T":
                            a1, a2 = slice(m * P, (m + 1) * P), slice(h * HALF, (h + 1) * HALF)
                            ins = mm3(pe, ps[:, n % 8, :], (wh[:, k, a1], wl[:, k, a1]), (xnh[:, k, a2], xnl[:, k, a2]),
                                      k == 0, k == DT - 1)
                        else:
                            a1 = slice(m * P, (m + 1) * P)
                            ins = mm3(pe, ps[:, n % 8, 0:2 * G1 * HD1], (xnh[:, k, a1], xnl[:, k, a1]),
                                      (wh[:, k, D:], wl[:, k, D:]), k == 0, k == DT - 1)
                    ins.then_inc(done, 1)
        c.clear()


def top_keys(dve, c_sem, idx, maskb, strip):
    n = 0

    def step(ins):
        nonlocal n
        n += 1
        ins.then_inc(c_sem[0], 1)
        dve.wait_ge(c_sem[0], n)

    top8 = c_sem[1]
    ROUNDS = TOPK // 8
    dve.tensor_copy(maskb[:, 0:P], strip[:, S - P:]).then_inc(c_sem[0], 1)
    n += 1
    for t in range(1, ST):
        row = idx[:, MASK_OFF[t]:MASK_OFF[t + 1]]
        diag = idx[:, MASK_OFF[t] + t * P:MASK_OFF[t + 1]]
        step(dve.tensor_tensor(diag, diag, strip[:, S - P:], ALU.add))
        with dve.Fori(0, ROUNDS) as r:
            dve.max(top8[:, :], row).then_inc(c_sem[0], 1)
            pause(dve, c_sem[0], r * 2 + (n + 1), c_sem[2])
            dve.match_replace(row, top8[:, :], row, TAKEN).then_inc(c_sem[0], 1)
            dve.wait_ge(c_sem[0], r * 2 + (n + 2))
        n += 2 * ROUNDS
        step(dve.tensor_scalar(maskb[:, MASK_OFF[t]:MASK_OFF[t + 1]], row, -2.0e38, MASKED, ALU.is_gt, ALU.mult))


def two_layers(nc, ins, consts, out):
    ident_d, strip_d, rope_d, cos_d, sin_d = consts
    scratch = lambda name, shape, dt=F32: nc.dram_tensor(name, shape, dt, kind="Internal").ap()
    wabs_d = scratch("wabs_d", (H // 2, QC, 2 * 3 * P))
    wvo_d = scratch("wvo_d", (H // 2, P, D))
    w1T_d = scratch("w1T_d", (D, F0))
    w3T_d = scratch("w3T_d", (D, F0))
    w2T_d = scratch("w2T_d", (F0, D))
    ctx0_d = scratch("ctx0_d", (H // 2, P, S))
    ctx1_d = scratch("ctx1_d", (G1, P, S))
    qd = scratch("qd", (2, D, S))
    kvd = scratch("kvd", (2, 2 * G1 * HD1, S))
    I = lambda n: ins[n]
    with ExitStack() as top:
        c = Ctx(nc, top)
        ps = top.enter_context(nc.psum_tensor("ps", [P, 8, HALF], F32))
        ident = c.sb("ident", [P, P])
        strip = c.sb("strip", [P, S])
        x = c.sb("x", [P, ST, D])
        c_in = c.sem("c_in")
        with nc.Block() as block:
            @block.sync
            def _(sp):
                sp.dma_start(ident[:, :], ident_d).then_inc(c_in, 16)
                sp.dma_start(strip[:, :], strip_d).then_inc(c_in, 16)
                sp.wait_ge(c_in, 32)
        fold_attention_weights(nc, ps, ident, I("L0_attn_q_b_w"), I("L0_attn_kv_b_w"), I("L0_attn_o_w"), wabs_d, wvo_d)
        fold_lora(nc, ps, ident, I("L0_ffn_w1"), I("L0_ffn_w3"), I("L0_ffn_w2"), I("L0_ffn_lora_A1"),
                  I("L0_ffn_lora_B1"), I("L0_ffn_lora_A3"), I("L0_ffn_lora_B3"), I("L0_ffn_lora_A2"),
                  I("L0_ffn_lora_B2"), w1T_d, w3T_d, w2T_d)
        with ExitStack() as layer0:
            c0 = Ctx(nc, layer0)
            maskb = c0.sb("maskb", [P, MASK_OFF[ST]], BF16)
            kh = c0.sb("kh", [P, S], F32R)
            kl = c0.sb("kl", [P, S], F32R)
            vst = c0.sb("vst", [P, ST, P], F32R)
            qlh = c0.sb("qlh", [QC, 2, S], F32R)
            qll = c0.sb("qll", [QC, 2, S], F32R)
            with ExitStack() as early:
                ce = Ctx(nc, early)
                xnh = ce.sb("xnh0", [P, DT, S], F32R)
                xnl = ce.sb("xnl0", [P, DT, S], F32R)
                ikh = ce.sb("ikh", [P, S], F32R)
                ikl = ce.sb("ikl", [P, S], F32R)
                aw = ce.sb("aw", [P, ST, IH])
                sg = ce.sb("sg", [P, ST, IH])
                idx = ce.sb("idx", [P, MASK_OFF[ST]])
                top8 = ce.sb("top8", [P, 8])
                found = ce.sem("top_step")
                layernorm(nc, "n0", ps, ident, x, xnh, xnl, I("L0_attn_hidden_states").rearrange("b s d -> (b s) d"))
                latents(nc, ps, ident, xnh, xnl, I("L0_attn_q_a_w"), I("L0_attn_kv_a_w"), I("L0_attn_idx_wk_w"),
                        I("L0_attn_idx_weights_w"), I("L0_attn_q_a_norm_w"), I("L0_attn_kv_a_norm_w"), rope_d,
                        qlh, qll, kh, kl, vst, ikh, ikl, aw, sg)
                index_scores(nc, ps, strip, xnh, xnl, I("L0_attn_idx_wq_w"), ikh, ikl, aw, sg, idx)
                ffn(nc, "f0", ps, xnh, xnl, x, F0, w1T_d, w3T_d, w2T_d, None, None,
                    beside=lambda dve: top_keys(dve, (found, top8, ce.sem("top_passed")), idx, maskb, strip))
            tables = (c0.sb("cosT", [P, S]), c0.sb("sinT", [P, S]))
            qwork = latent_queries(nc, ps, ident, (qlh, qll), wabs_d, cos_d, sin_d, tables)

            def passes0(i, ahead, a):
                qh, ql = qwork["bufs"]
                return [(lambda at: qh[:, a, at], lambda k0, k1: kh[:, k0:k1]),
                        (lambda at: qh[:, a, at], lambda k0, k1: kl[:, k0:k1]),
                        (lambda at: ql[:, a, at], lambda k0, k1: kh[:, k0:k1])]
            attention(nc, "a0", ps, H // 2, 2, passes0, lambda t: maskb[:, MASK_OFF[t]:MASK_OFF[t + 1]], QKD ** -0.5,
                      lambda j: vst[:, j, :], qwork, ctx0_d, 2)

            def load_wvo(sp, k, dst, sem):
                sp.dma_start(dst, wvo_d[k]).then_inc(sem, 16)
            project_out(nc, "o0", ps, x, H // 2, ctx0_d, load_wvo, 1, None)
        with ExitStack() as layer1:
            c1 = Ctx(nc, layer1)
            xnh = c1.sb("xnh1", [P, DT, S], F32R)
            xnl = c1.sb("xnl1", [P, DT, S], F32R)
            layernorm(nc, "n1", ps, ident, x, xnh, xnl)
            with ExitStack() as att:
                ca = Ctx(nc, att)
                vs_all = ca.sb("vs_all", [P, ST, G1, 2 * HD1], F32R)
                vg = ca.sb("vg", [P, ST, REP1, 2 * HD1], F32R)
                layer1_qkv(nc, ps, xnh, xnl, I("L1_attn_Wq"), I("L1_attn_Wkv"), qd, kvd, vs_all)
                qwork = stacked_queries(nc, ps, ident, vs_all, vg, qd, kvd)

                def passes1(i, ahead, a):
                    qst, kst = qwork["bufs"]
                    return [(lambda at: qst[:, a, at],
                             lambda k0, k1: kst[:, bass.ds(i + ahead, 1), k0:k1].rearrange("p o n -> p (o n)"))]
                attention(nc, "a1", ps, G1, REP1, passes1, lambda t: strip[:, S - (t + 1) * P:], HD1 ** -0.5,
                          lambda j: vg[:, j, :, :].rearrange("p r n -> p (r n)"), qwork, ctx1_d, 1)
            wo = I("L1_attn_Wo")

            def load_wo(sp, k, dst, sem):
                for h in range(REP1):
                    for l in range(2):
                        r0 = 32 * h + HD1 * l
                        sp.dma_start(dst[r0:r0 + HD1, :], wo[bass.ds(k * (REP1 * HD1) + h * HD1, HD1), :]).then_inc(sem, 16)
            project_out(nc, "o1", ps, x, G1, ctx1_d, load_wo, 2 * REP1, I("L1_attn_bo"))
            ffn(nc, "f1", ps, xnh, xnl, x, F1, I("L1_ffn_inter_w"), None, I("L1_ffn_output_w"), I("L1_ffn_inter_b"),
                I("L1_ffn_output_b"), out_d=out.rearrange("b s d -> (b s) d"))


_INS = ['L0_attn_hidden_states', 'L0_attn_q_a_w', 'L0_attn_q_a_norm_w', 'L0_attn_q_b_w', 'L0_attn_kv_a_w',
        'L0_attn_kv_a_norm_w', 'L0_attn_kv_b_w', 'L0_attn_o_w', 'L0_attn_idx_wq_w', 'L0_attn_idx_wk_w',
        'L0_attn_idx_weights_w', 'L0_ffn_w1', 'L0_ffn_w3', 'L0_ffn_w2', 'L0_ffn_lora_A1', 'L0_ffn_lora_B1',
        'L0_ffn_lora_A3', 'L0_ffn_lora_B3', 'L0_ffn_lora_A2', 'L0_ffn_lora_B2', 'L1_attn_Wq', 'L1_attn_Wkv',
        'L1_attn_Wo', 'L1_attn_bo', 'L1_ffn_inter_w', 'L1_ffn_inter_b', 'L1_ffn_output_w', 'L1_ffn_output_b']


def constants():
    ident = np.eye(P, dtype=np.float32)
    strip = np.zeros((P, S), np.float32)
    strip[:, S - P:] = np.where(np.arange(P)[:, None] >= np.arange(P)[None, :], 0.0, MASKED)
    inv_freq = (np.float32(1.0) / np.float32(10000.0) ** (np.arange(0, ROPE, 2, dtype=np.float32) / np.float32(ROPE)))
    ang = (np.arange(S, dtype=np.float32)[:, None] * inv_freq[None, :].astype(np.float32)).astype(np.float64)
    cos, sin = np.cos(ang).astype(np.float32), np.sin(ang).astype(np.float32)
    rope = np.stack([cos, sin], axis=1)
    cosT = np.concatenate([np.ones((64, S), np.float32), cos.T, cos.T])
    sinT = np.concatenate([-sin.T, sin.T, -sin.T, sin.T])
    return {"c_ident": ident, "c_strip": strip, "c_rope": rope, "c_cosT": cosT, "c_sinT": sinT}


def kernel(**inputs):
    import concourse.bacc as _bacc
    from concourse.bass_utils import run_bass_kernel_spmd as _run

    nc = _bacc.Bacc("TRN2", target_bir_lowering=False, num_devices=1)
    arrays, args, consts = {}, {}, []
    for name in _INS:
        a = np.ascontiguousarray(inputs[name])
        arrays[f"in_{name}"] = a
        args[name] = nc.dram_tensor(f"in_{name}", a.shape, mybir.dt.from_np(a.dtype), kind="ExternalInput").ap()
    for name, a in constants().items():
        a = np.ascontiguousarray(a)
        arrays[name] = a
        consts.append(nc.dram_tensor(name, a.shape, F32, kind="ExternalInput").ap())
    out = nc.dram_tensor("out_0_dram", (1, S, D), F32, kind="ExternalOutput").ap()
    two_layers(nc, args, consts, out)
    r = _run(nc, [arrays], core_ids=[0])
    return r.results[0]["out_0_dram"]
```

```python
from contextlib import ExitStack

import numpy as np
import concourse.bass as bass
from concourse import mybir

F32 = mybir.dt.float32
F32R = mybir.dt.float32r
BF16 = mybir.dt.bfloat16
ALU = mybir.AluOpType
ACT = mybir.ActivationFunctionType
AX_X = mybir.AxisListType.X

P = 128
S = 1024
D = 512
ST = S // P
DT = D // P
HALF = 512
PAIR = 2 * P
EPS = 1e-5

H = 32
NOPE, ROPE, VD = 128, 64, 128
QKD = NOPE + ROPE
QR, KVR = 192, 64
QC = QR // 2
IH, ID, TOPK = 16, 128, 128
LAT = QR + KVR + ROPE + ID + IH
C_KV, C_PE, C_IK, C_IW = QR, QR + KVR, QR + KVR + ROPE, QR + KVR + ROPE + ID

F0, R0 = 1376, 16
LORA_SCALE = 2.0
F1 = 2048
G1, HD1 = 8, 16
REP1 = H // G1

MASKED = -1.0e30
START = 1
TAKEN = -3.0e38
MASK_OFF = [P * t * (t + 1) // 2 for t in range(ST + 1)]


def f32(ap):
    return ap.bitcast(F32)


class Ctx:
    finished = []

    def __init__(self, nc, stack):
        self.nc, self.stack, self.mine, self.sem_stack = nc, stack, [], ExitStack()

    def sb(self, name, shape, dt=F32):
        return self.stack.enter_context(self.nc.sbuf_tensor(name, shape, dt))

    def sem(self, name):
        s = self.sem_stack.enter_context(self.nc.semaphore(name))
        self.mine.append(s)
        return s

    def sems(self, name, n):
        return [self.sem(f"{name}{i}") for i in range(n)]

    def begin(self):
        old = [s for c in Ctx.finished for s in c.mine]
        with self.nc.Block() as block:
            def share(eng, k):
                for s in old[k::3]:
                    eng.sem_clear(s)
                for s in self.mine[k::3]:
                    eng.sem_inc(s, START)

            @block.gpsimd
            def _(pool):
                share(pool, 0)

            @block.scalar
            def _(act):
                share(act, 1)

            @block.vector
            def _(dve):
                share(dve, 2)
        for c in Ctx.finished:
            c.sem_stack.close()
        Ctx.finished = []

    def finish(self):
        Ctx.finished.append(self)


def pause(eng, sem, value, passed):
    eng.wait_ge(sem, START + value)
    eng.sem_inc(passed, 1)


def mm3(pe, out, left, right, start, stop):
    (lh, ll), (rh, rl) = left, right
    pe.matmul(out, lh, rh, start=start, stop=False, skip_group_check=True)
    pe.matmul(out, lh, rl, start=False, stop=False, skip_group_check=True)
    return pe.matmul(out, ll, rh, start=False, stop=stop, skip_group_check=True)


def fold_attention_weights(nc, ps, ident, q_b_w, kv_b_w, o_w, wabs_d, wvo_d):
    NP = H // 2
    with ExitStack() as st:
        c = Ctx(nc, st)
        wq = c.sb("fw_wq", [QC, 4, 2, 2, QKD])
        wkv = c.sb("fw_wkv", [KVR, 4, 2, NOPE + VD])
        wo = c.sb("fw_wo", [P, 4, 2, D])
        wT = c.sb("fw_wT", [P, 4, 2, 320])
        wabs = c.sb("fw_wabs", [QC, 4, 2, 3, P])
        wvo = c.sb("fw_wvo", [P, 4, D])
        raw_in, turned, wT_done, folded, abs_done, vo_done, pe_copied, abs_out, vo_out = (
            c.sems("fw_" + n, 4) for n in ("raw_in", "turned", "wT_done", "folded", "abs_done", "vo_done",
                                           "pe_copied", "abs_out", "vo_out"))
        passed_sp, passed_act, passed_pool = (c.sem("fw_passed_" + n) for n in ("sp", "act", "pool"))
        wq_v = q_b_w.rearrange("(c p) (j a n) -> j p c a n", c=2, a=2, n=QKD)
        wkv_v = kv_b_w.rearrange("p (j a n) -> j p a n", a=2, n=NOPE + VD)
        wo_v = o_w.rearrange("(j a p) n -> j p a n", a=2, p=VD)
        c.begin()
        with nc.Block() as block:
            @block.sync
            def _(sp):
                with sp.Fori(0, NP // 4) as i:
                    for s in range(4):
                        pause(sp, folded[s], i * 2, passed_sp)
                        pause(sp, pe_copied[s], i, passed_sp)
                        for c_ in range(2):
                            sp.dma_start(wq[:, s, c_], wq_v[i * 4 + s][:, c_]).then_inc(raw_in[s], 16)
                        sp.dma_start(wkv[:, s], wkv_v[i * 4 + s]).then_inc(raw_in[s], 16)
                        sp.dma_start(wo[:, s], wo_v[i * 4 + s]).then_inc(raw_in[s], 16)
                for s in range(4):
                    sp.wait_ge(abs_out[s], START + 16 * (NP // 4))
                    sp.wait_ge(vo_out[s], START + 16 * (NP // 4))

            @block.tensor
            def _(pe):
                with pe.Fori(0, NP // 4) as i:
                    for group in ((0, 1), (2, 3)):
                        for s in group:
                            pe.wait_ge(raw_in[s], START + i * 64 + 64)
                            before, n = ((s + 2) % 4, i + s // 2)
                            pe.wait_ge(wT_done[before], START + n * 2)
                            for a in range(2):
                                b = 4 * (s % 2) + a
                                for k in range(2):
                                    pe.transpose(ps[:, b, k * QC:(k + 1) * QC], wq[:, s, k, a, 0:NOPE], ident[0:QC, 0:QC])
                                pe.transpose(ps[:, b, 192:256], wkv[:, s, a, 0:NOPE], ident[0:KVR, 0:KVR])
                                pe.transpose(ps[:, b, 256:320], wkv[:, s, a, NOPE:], ident[0:KVR, 0:KVR]).then_inc(
                                    turned[s], 1)
                        for s in group:
                            before, n = ((s + 2) % 4, i + s // 2)
                            pe.wait_ge(abs_done[before], START + n)
                            pe.wait_ge(vo_done[before], START + n)
                            for a in range(2):
                                pe.wait_ge(wT_done[s], START + i * 2 + a + 1)
                                for k in range(2):
                                    pe.matmul(ps[0:QC, 4 * (s % 2) + 2, (a * 2 + k) * 64:(a * 2 + k + 1) * 64],
                                              wT[:, s, a, k * QC:(k + 1) * QC], wT[:, s, a, 192:256], start=True, stop=True)
                                pe.matmul(ps[64 * a:64 * a + 64, 4 * (s % 2) + 3, :], wT[:, s, a, 256:320], wo[:, s, a, :],
                                          start=True, stop=True).then_inc(folded[s], 1)

            @block.scalar
            def _(act):
                with act.Fori(0, NP // 4) as i:
                    for group in ((0, 1), (2, 3)):
                        for s in group:
                            act.wait_ge(folded[s], START + i * 2)
                            for a in range(2):
                                act.wait_ge(turned[s], START + i * 2 + a + 1)
                                act.copy(wT[:, s, a, :], ps[:, 4 * (s % 2) + a, 0:320]).then_inc(wT_done[s], 1)
                        for s in group:
                            act.wait_ge(folded[s], START + i * 2 + 2)
                            act.wait_ge(vo_out[s], START + i * 16)
                            act.copy(wvo[:, s], ps[:, 4 * (s % 2) + 3, :]).then_inc(vo_done[s], 1)
                        for s in group:
                            act.wait_ge(pe_copied[s], START + i + 1)
                            pause(act, abs_done[s], i + 1, passed_act)
                            act.dma_start(wabs_d[i * 4 + s], wabs[:, s].rearrange("p c b n -> p (c b n)")).then_inc(abs_out[s], 16)
                            pause(act, vo_done[s], i + 1, passed_act)
                            act.dma_start(wvo_d[i * 4 + s], wvo[:, s]).then_inc(vo_out[s], 16)

            @block.vector
            def _(dve):
                with dve.Fori(0, NP // 4) as i:
                    for group in ((0, 1), (2, 3)):
                        for s in group:
                            dve.wait_ge(folded[s], START + i * 2 + 2)
                            dve.wait_ge(abs_out[s], START + i * 16)
                            for a in range(2):
                                ins = dve.tensor_copy(wabs[:, s, :, a, 0:64],
                                                      ps[0:QC, 4 * (s % 2) + 2, a * 128:(a + 1) * 128].rearrange("p (k n) -> p k n", k=2))
                            ins.then_inc(abs_done[s], 1)

            @block.gpsimd
            def _(pool):
                with pool.Fori(0, NP // 4) as i:
                    for s in range(4):
                        pool.wait_ge(raw_in[s], START + i * 64 + 64)
                        pause(pool, abs_out[s], i * 16, passed_pool)
                        for a in range(2):
                            pair = wq[:, s, :, a, NOPE:].rearrange("p c (n e) -> p c e n", e=2)
                            pool.tensor_copy(wabs[:, s, :, a, 64:96], pair[:, :, 0, :])
                            pool.tensor_copy(wabs[:, s, :, a, 96:128], pair[:, :, 1, :])
                            pool.tensor_copy(wabs[:, s, :, 2, 64 * a:64 * a + 32], pair[:, :, 1, :])
                            ins = pool.tensor_copy(wabs[:, s, :, 2, 64 * a + 32:64 * a + 64], pair[:, :, 0, :])
                        ins.then_inc(pe_copied[s], 1)
        c.finish()


def fold_lora(nc, ps, ident, w1, w3, w2, A1, B1, A3, B3, A2, B2, w1T_d, w3T_d, w2T_d):
    NF = F0 // P
    LASTN = F0 - NF * P
    with ExitStack() as st:
        c = Ctx(nc, st)
        wr = c.sb("fl_w", [P, 4, 2, D])
        w2r = c.sb("fl_w2", [P, 4, DT, P])
        br = c.sb("fl_b", [P, 4, 2, R0])
        a13 = c.sb("fl_a13", [R0, 2, D])
        a2 = c.sb("fl_a2", [R0, 4, P])
        b2 = c.sb("fl_b2", [P, DT, R0])
        b2T = c.sb("fl_b2T", [R0, D])
        bT = c.sb("fl_bT", [R0, 4, 2, P])
        wT = c.sb("fl_wT", [P, 4, 2, DT, P])
        w2T = c.sb("fl_w2T", [P, 4, D])
        once_in, b2_turned, b2_done = (c.sem("fl_" + n) for n in ("once_in", "b2_turned", "b2_done"))
        raw_in, b_turned, bT_done, summed, evac_a, evac_d, stored = (
            c.sems("fl_" + n, 4) for n in ("raw_in", "b_turned", "bT_done", "summed", "evac_a", "evac_d", "stored"))
        passed_sp, passed_act = c.sem("fl_passed_sp"), c.sem("fl_passed_act")
        w1T_v = w1T_d.rearrange("(k p) n -> p k n", p=P)
        w3T_v = w3T_d.rearrange("(k p) n -> p k n", p=P)
        w2_v = w2.rearrange("(k p) n -> p k n", p=P)

        def bank(b):
            return ps[:, b, :].rearrange("p (k n) -> p k n", k=DT)

        def chunks(eng, body):
            with eng.Fori(0, NF // 4) as i:
                for s0 in (0, 2):
                    body(i, [(s, i * (4 * P) + s * P, P) for s in (s0, s0 + 1)])
            rest = [(k % 4, k * P, P) for k in range(NF // 4 * 4, NF)] + [(NF % 4, NF * P, LASTN)]
            for k in range(0, len(rest), 2):
                body(NF // 4, rest[k:k + 2])

        c.begin()
        with nc.Block() as block:
            @block.sync
            def _(sp):
                sp.dma_start(a13[:, 0], A1).then_inc(once_in, 16)
                sp.dma_start(a13[:, 1], A3).then_inc(once_in, 16)
                sp.dma_start(b2[:, :, :], B2.rearrange("(k p) r -> p k r", p=P)).then_inc(once_in, 16)

                def body(i, slots):
                    for s, c0, n in slots:
                        at = bass.ds(c0, n)
                        pause(sp, summed[s], i * 3, passed_sp)
                        sp.dma_start(wr[0:n, s, 0], w1[at, :]).then_inc(raw_in[s], 16)
                        sp.dma_start(wr[0:n, s, 1], w3[at, :]).then_inc(raw_in[s], 16)
                        sp.dma_start(w2r[:, s, :, 0:n], w2_v[:, :, at]).then_inc(raw_in[s], 16)
                        sp.dma_start(a2[:, s, 0:n], A2[:, at]).then_inc(raw_in[s], 16)
                        sp.dma_start(br[0:n, s, 0], B1[at, :]).then_inc(raw_in[s], 16)
                        sp.dma_start(br[0:n, s, 1], B3[at, :]).then_inc(raw_in[s], 16)
                chunks(sp, body)
                for s in range(4):
                    sp.wait_ge(stored[s], START + 48 * (NF // 4 + (s <= NF % 4)))

            @block.tensor
            def _(pe):
                pe.wait_ge(once_in, START + 48)
                for k in range(DT):
                    ins = pe.transpose(ps[0:R0, 0, k * P:(k + 1) * P], b2[:, k, :], ident[:, :])
                ins.then_inc(b2_turned, 1)
                pe.wait_ge(b2_done, START + 1)

                def body(i, slots):
                    for s, c0, n in slots:
                        before, n_ = ((s + 2) % 4, i + s // 2)
                        pe.wait_ge(bT_done[before], START + n_)
                        pe.wait_ge(raw_in[s], START + i * 96 + 96)
                        for m in range(2):
                            ins = pe.transpose(ps[0:R0, 4 * (s % 2), m * P:m * P + n], br[0:n, s, m, :], ident[0:n, 0:n])
                        ins.then_inc(b_turned[s], 1)
                    for s, c0, n in slots:
                        before, n_ = ((s + 2) % 4, i + s // 2)
                        pe.wait_ge(evac_a[before], START + n_ * 2)
                        pe.wait_ge(evac_d[before], START + n_)
                        pe.wait_ge(bT_done[s], START + i + 1)
                        for m in range(2):
                            for k in range(DT):
                                o = ps[:, 4 * (s % 2) + 1 + m, k * P:k * P + n]
                                pe.matmul(o, wr[0:n, s, m, k * P:(k + 1) * P], ident[0:n, 0:n], start=True, stop=False,
                                          is_transpose=True, skip_group_check=True)
                                ins = pe.matmul(o, a13[:, m, k * P:(k + 1) * P], bT[:, s, m, 0:n], start=False, stop=True,
                                                skip_group_check=True)
                            ins.then_inc(summed[s], 1)
                        for k in range(DT):
                            o = ps[0:n, 4 * (s % 2) + 3, k * P:(k + 1) * P]
                            pe.matmul(o, w2r[:, s, k, 0:n], ident[:, :], start=True, stop=False,
                                      is_transpose=True, skip_group_check=True)
                            ins = pe.matmul(o, a2[:, s, 0:n], b2T[:, k * P:(k + 1) * P], start=False, stop=True,
                                            skip_group_check=True)
                        ins.then_inc(summed[s], 1)
                chunks(pe, body)

            @block.scalar
            def _(act):
                act.wait_ge(b2_turned, START + 1)
                act.mul(b2T[:, :], ps[0:R0, 0, :], LORA_SCALE).then_inc(b2_done, 1)

                def body(i, slots):
                    for s, c0, n in slots:
                        act.wait_ge(b_turned[s], START + i + 1)
                        act.mul(bT[:, s, :, 0:n], ps[0:R0, 4 * (s % 2), 0:2 * P].rearrange("r (m n) -> r m n", m=2)[:, :, 0:n],
                                LORA_SCALE).then_inc(bT_done[s], 1)
                    for s, c0, n in slots:
                        act.wait_ge(stored[s], START + i * 48)
                        act.wait_ge(summed[s], START + i * 3 + 1)
                        act.copy(wT[:, s, 0, :, 0:n], bank(4 * (s % 2) + 1)[:, :, 0:n]).then_inc(evac_a[s], 1)
                        act.wait_ge(summed[s], START + i * 3 + 3)
                        act.copy(w2T[0:n, s], ps[0:n, 4 * (s % 2) + 3, :]).then_inc(evac_a[s], 1)
                    for s, c0, n in slots:
                        at = bass.ds(c0, n)
                        act.wait_ge(evac_d[s], START + i + 1)
                        pause(act, evac_a[s], i * 2 + 2, passed_act)
                        act.dma_start(w1T_v[:, :, at], wT[:, s, 0, :, 0:n]).then_inc(stored[s], 16)
                        act.dma_start(w3T_v[:, :, at], wT[:, s, 1, :, 0:n]).then_inc(stored[s], 16)
                        act.dma_start(w2T_d[at, :], w2T[0:n, s]).then_inc(stored[s], 16)
                chunks(act, body)

            @block.vector
            def _(dve):
                def body(i, slots):
                    for s, c0, n in slots:
                        dve.wait_ge(stored[s], START + i * 48)
                        dve.wait_ge(summed[s], START + i * 3 + 2)
                        dve.tensor_copy(wT[:, s, 1, :, 0:n], bank(4 * (s % 2) + 2)[:, :, 0:n]).then_inc(evac_d[s], 1)
                chunks(dve, body)
        c.finish()


def layernorm(nc, tag, ps, ident, x, xnh, xnl, x_dram=None):
    with ExitStack() as st:
        c = Ctx(nc, st)
        xn = c.sb(tag + "_xn", [P, ST, D])
        stats = c.sb(tag + "_stats", [P, ST, 6])
        mv = c.sb(tag + "_mv", [P, ST, 2])
        std = c.sb(tag + "_std", [P, ST])
        rstd = c.sb(tag + "_rstd", [P, ST])
        x_in, stat, var_done, std_done, rstd_done, xn_done, turned, hi_done = (
            c.sem(f"{tag}_{n}") for n in ("x_in", "stat", "var_done", "std_done", "rstd_done", "xn_done", "turned",
                                          "hi_done"))
        lo_done = c.sems(tag + "_lo_done", 2)
        c.begin()
        with nc.Block() as block:
            @block.sync
            def _(sp):
                if x_dram is not None:
                    for t in range(ST):
                        sp.dma_start(x[:, t], x_dram[t * P:(t + 1) * P, :]).then_inc(x_in, 16)

            @block.vector
            def _(dve):
                for t in range(ST):
                    if x_dram is not None:
                        dve.wait_ge(x_in, START + 16 * ST)
                    dve.bn_stats(stats[:, t], x[:, t]).then_inc(stat, 1)
                dve.wait_ge(stat, START + ST)
                for t in range(ST):
                    dve.bn_aggr(mv[:, t], stats[:, t]).then_inc(stat, 1)
                dve.wait_ge(stat, START + 2 * ST)
                dve.tensor_scalar_add(std[:, :], mv[:, :, 1], EPS).then_inc(var_done, 1)
                dve.wait_ge(std_done, START + 1)
                dve.reciprocal(rstd[:, :], std[:, :]).then_inc(rstd_done, 1)
                dve.wait_ge(rstd_done, START + 1)
                for t in range(ST):
                    dve.tensor_scalar(xn[:, t], x[:, t], mv[:, t, 0:1], rstd[:, t:t + 1], ALU.subtract,
                                      ALU.mult).then_inc(xn_done, 1)
                for t in range(ST):
                    dve.wait_ge(hi_done, START + t + 1)
                    at = slice(t * P, (t + 1) * P)
                    dve.tensor_tensor(xnl[:, :, at], bank4(ps, t % 2), f32(xnh[:, :, at]),
                                      ALU.subtract).then_inc(lo_done[t % 2], 1)

            @block.scalar
            def _(act):
                act.wait_ge(var_done, START + 1)
                act.activation(std[:, :], std[:, :], ACT.Sqrt).then_inc(std_done, 1)
                for t in range(ST):
                    act.wait_ge(turned, START + t + 1)
                    act.copy(xnh[:, :, t * P:(t + 1) * P], bank4(ps, t % 2)).then_inc(hi_done, 1)

            @block.tensor
            def _(pe):
                for t in range(ST):
                    pe.wait_ge(xn_done, START + t + 1)
                    if t >= 2:
                        pe.wait_ge(lo_done[t % 2], START + t // 2)
                    for k in range(DT):
                        ins = pe.transpose(ps[:, t % 2, k * P:(k + 1) * P], xn[:, t, k * P:(k + 1) * P], ident[:, :])
                    ins.then_inc(turned, 1)
        c.finish()


def bank4(ps, b):
    return ps[:, b, :].rearrange("p (k n) -> p k n", k=4)


def latents(nc, ps, ident, xnh, xnl, q_a_w, kv_a_w, wk_w, ww_w, qn_w, kvn_w, rope_t, qlh, qll, kh, kl, vst, ikh, ikl,
            aw, sg):
    with ExitStack() as st:
        c = Ctx(nc, st)
        w = c.sb("la_w", [P, DT, LAT])
        wh = c.sb("la_wh", [P, DT, LAT], F32R)
        wl = c.sb("la_wl", [P, DT, LAT], F32R)
        lat = c.sb("la_lat", [P, ST, LAT])
        sq = c.sb("la_sq", [P, ST, QR + KVR])
        ss = c.sb("la_ss", [P, 2, ST])
        rs = c.sb("la_rs", [P, 2, ST])
        qn = c.sb("la_qn", [P, QR])
        kvn = c.sb("la_kvn", [P, KVR])
        rope = c.sb("la_rope", [P, ST, 2, ROPE // 2])
        ql = c.sb("la_ql", [P, ST, QR])
        kc = c.sb("la_kc", [P, ST, P])
        rot = c.sb("la_rot", [P, 4, ST, ROPE // 2])
        w_in, c_in, wh_done, wl_done, latted, lat_done, dve_step, ss_done, std_done, tok_done, turned, hi_done, vh_done = (
            c.sem("la_" + n) for n in ("w_in", "c_in", "wh_done", "wl_done", "latted", "lat_done", "dve_step",
                                       "ss_done", "std_done", "tok_done", "turned", "hi_done", "vh_done"))
        lo_done = c.sems("la_lo_done", 2)
        c.begin()
        with nc.Block() as block:
            @block.sync
            def _(sp):
                for src, c0, n in ((q_a_w, 0, QR), (kv_a_w, C_KV, KVR + ROPE), (wk_w, C_IK, ID), (ww_w, C_IW, IH)):
                    sp.dma_start(w[:, :, c0:c0 + n], src.rearrange("(k p) n -> p k n", p=P)).then_inc(w_in, 16)
                sp.dma_start(qn[:, :], qn_w.partition_broadcast(P)).then_inc(c_in, 16)
                sp.dma_start(kvn[:, :], kvn_w.partition_broadcast(P)).then_inc(c_in, 16)
                sp.dma_start(rope[:, :, :, :], rope_t.rearrange("(t p) e n -> p t e n", p=P)).then_inc(c_in, 16)

            @block.gpsimd
            def _(pool):
                pool.wait_ge(wh_done, START + 1)
                pool.tensor_tensor(wl[:, :, :], w[:, :, :], f32(wh[:, :, :]), ALU.subtract).then_inc(wl_done, 1)

            @block.tensor
            def _(pe):
                pe.wait_ge(wl_done, START + 1)
                for t in range(ST):
                    at = slice(t * P, (t + 1) * P)
                    for k in range(DT):
                        ins = mm3(pe, ps[:, t, 0:LAT], (xnh[:, k, at], xnl[:, k, at]), (wh[:, k], wl[:, k]),
                                  k == 0, k == DT - 1)
                    ins.then_inc(latted, 1)
                pe.wait_ge(tok_done, START + 1)
                for t in range(ST):
                    if t >= 2:
                        pe.wait_ge(lo_done[t % 2], START + t // 2)
                    b = t % 2
                    pe.transpose(ps[:, b, 0:P], kc[:, t], ident[:, :])
                    pe.transpose(ps[:, b, P:2 * P], lat[:, t, C_IK:C_IK + ID], ident[:, :])
                    for k in range(2):
                        ins = pe.transpose(ps[0:QC, b, (2 + k) * P:(3 + k) * P], ql[:, t, k * QC:(k + 1) * QC],
                                           ident[:, :])
                    ins.then_inc(turned, 1)

            @block.scalar
            def _(act):
                act.wait_ge(w_in, START + 64)
                act.copy(wh[:, :, :], w[:, :, :]).then_inc(wh_done, 1)
                for t in range(ST):
                    act.wait_ge(latted, START + t + 1)
                    act.copy(lat[:, t], ps[:, t, 0:LAT]).then_inc(lat_done, 1)
                act.wait_ge(ss_done, START + 1)
                act.activation(ss[:, :, :], ss[:, :, :], ACT.Sqrt).then_inc(std_done, 1)
                act.wait_ge(tok_done, START + 1)
                act.copy(vst[:, :, 0:KVR], kc[:, :, 0:KVR]).then_inc(vh_done, 1)
                for t in range(ST):
                    at = slice(t * P, (t + 1) * P)
                    act.wait_ge(turned, START + t + 1)
                    act.copy(kh[:, at], ps[:, t % 2, 0:P])
                    act.copy(ikh[:, at], ps[:, t % 2, P:2 * P])
                    act.copy(qlh[:, :, at], ps[0:QC, t % 2, 2 * P:].rearrange("p (k n) -> p k n", k=2)).then_inc(hi_done, 1)

            @block.vector
            def _(dve):
                n = 0

                def step(ins):
                    nonlocal n
                    n += 1
                    ins.then_inc(dve_step, 1)
                    dve.wait_ge(dve_step, START + n)

                dve.wait_ge(lat_done, START + ST)
                dve.wait_ge(c_in, START + 48)
                step(dve.tensor_tensor(sq[:, :, :], lat[:, :, 0:QR + KVR], lat[:, :, 0:QR + KVR], ALU.mult))
                dve.tensor_reduce(ss[:, 0], sq[:, :, 0:QR], AX_X, ALU.add)
                step(dve.tensor_reduce(ss[:, 1], sq[:, :, QR:], AX_X, ALU.add))
                dve.tensor_scalar(ss[:, 0], ss[:, 0], 1.0 / QR, EPS, ALU.mult, ALU.add)
                dve.tensor_scalar(ss[:, 1], ss[:, 1], 1.0 / KVR, EPS, ALU.mult, ALU.add).then_inc(ss_done, 1)
                dve.wait_ge(std_done, START + 1)
                step(dve.reciprocal(rs[:, :, :], ss[:, :, :]))
                for t in range(ST):
                    dve.scalar_tensor_tensor(out=ql[:, t], in0=lat[:, t, 0:QR], scalar=rs[:, 0, t:t + 1], in1=qn[:, :],
                                             op0=ALU.mult, op1=ALU.mult)
                    dve.scalar_tensor_tensor(out=kc[:, t, 0:KVR], in0=lat[:, t, C_KV:C_KV + KVR],
                                             scalar=rs[:, 1, t:t + 1], in1=kvn[:, :], op0=ALU.mult, op1=ALU.mult)
                pe_pair = lat[:, :, C_PE:C_PE + ROPE].rearrange("p t (n e) -> p t n e", e=2)
                for j, (e, sc) in enumerate(((0, 0), (1, 1), (1, 0), (0, 1))):
                    ins = dve.tensor_tensor(rot[:, j], pe_pair[:, :, :, e], rope[:, :, sc, :], ALU.mult)
                step(ins)
                dve.tensor_tensor(kc[:, :, 64:96], rot[:, 0], rot[:, 1], ALU.subtract)
                dve.tensor_tensor(kc[:, :, 96:128], rot[:, 2], rot[:, 3], ALU.add)
                iw = lat[:, :, C_IW:C_IW + IH]
                dve.tensor_scalar(sg[:, :, :], iw, 0.0, 2.0, ALU.is_ge, ALU.mult)
                dve.tensor_scalar(aw[:, :, :], iw, IH ** -0.5 * ID ** -0.5, None, ALU.mult).then_inc(tok_done, 1)
                dve.wait_ge(tok_done, START + 1)
                step(dve.tensor_scalar(sg[:, :, :], sg[:, :, :], -1.0, None, ALU.add))
                dve.tensor_tensor(aw[:, :, :], aw[:, :, :], sg[:, :, :], ALU.mult)
                dve.wait_ge(vh_done, START + 1)
                dve.tensor_tensor(vst[:, :, KVR:], kc[:, :, 0:KVR], f32(vst[:, :, 0:KVR]), ALU.subtract)
                for t in range(ST):
                    at = slice(t * P, (t + 1) * P)
                    dve.wait_ge(hi_done, START + t + 1)
                    dve.tensor_tensor(kl[:, at], ps[:, t % 2, 0:P], f32(kh[:, at]), ALU.subtract)
                    dve.tensor_tensor(ikl[:, at], ps[:, t % 2, P:2 * P], f32(ikh[:, at]), ALU.subtract)
                    dve.tensor_tensor(qll[:, :, at], ps[0:QC, t % 2, 2 * P:].rearrange("p (k n) -> p k n", k=2),
                                      f32(qlh[:, :, at]), ALU.subtract).then_inc(lo_done[t % 2], 1)
        c.finish()


def index_scores(nc, ps, xnh, xnl, wq_w, ikh, ikl, aw, sg, idx):
    with ExitStack() as st:
        c = Ctx(nc, st)
        w = c.sb("ix_w", [P, 2, DT, P])
        wh = c.sb("ix_wh", [P, 2, DT, P], F32R)
        wl = c.sb("ix_wl", [P, 2, DT, P], F32R)
        iqh = c.sb("ix_iqh", [P, 2, S], F32R)
        iql = c.sb("ix_iql", [P, 2, S], F32R)
        awc = c.sb("ix_awc", [P, 2, ST])
        sgc = c.sb("ix_sgc", [P, 2, ST])
        r = c.sb("ix_r", [P, 2, S])
        wh_done, wl_done, projected, iqh_done, iql_done, wc_done, scored = (
            c.sem("ix_" + n) for n in ("wh_done", "wl_done", "projected", "iqh_done", "iql_done", "wc_done", "scored"))
        raw_in = c.sems("ix_raw_in", 2)
        relu_done = c.sems("ix_relu_done", 2)
        added = c.sems("ix_added", 2)
        added_zero = c.sem("ix_added_zero")
        w_v = wq_w.rearrange("(k p) (j a n) -> j p a k n", p=P, a=2, n=ID)
        NP = IH // 2
        PIECES = (2, 2, 1, 1, 1, 1, 0, 0)
        SPLIT_AT = 6
        slots = [ps[:, 2 * k:2 * k + 2, :].rearrange("p b n -> p (b n)") for k in range(2)]
        ps_iq = ps[:, 6:8, :].rearrange("p b n -> p (b n)")

        def pairs(eng, body):
            with eng.Fori(0, NP - 1) as i:
                body(i, False)
            body(NP - 1, True)

        c.begin()
        with nc.Block() as block:
            @block.sync
            def _(sp):
                with sp.Fori(0, NP) as i:
                    for a in range(2):
                        sp.wait_ge(wl_done, START + i * 2)
                        for k in range(DT):
                            sp.dma_start(w[:, a, k], w_v[i][:, a, k]).then_inc(raw_in[a], 16)

            @block.gpsimd
            def _(pool):
                with pool.Fori(0, NP) as i:
                    for a in range(2):
                        pool.wait_ge(wh_done, START + i * 2 + a + 1)
                        pool.tensor_tensor(wl[:, a], w[:, a], f32(wh[:, a]), ALU.subtract).then_inc(wl_done, 1)

            @block.tensor
            def _(pe):
                def project(n, a, piece):
                    h, k = divmod(piece, DT)
                    if piece == 0:
                        pe.wait_ge(wl_done, START + n + 1)
                    at = slice(h * HALF, (h + 1) * HALF)
                    ins = mm3(pe, ps_iq[:, at], (wh[:, a, k], wl[:, a, k]), (xnh[:, k, at], xnl[:, k, at]),
                              k == 0, k == DT - 1)
                    if piece == 2 * DT - 1:
                        ins.then_inc(projected, 1)

                def score(i, a, more):
                    pe.wait_ge(iql_done, START + i * 2 + a + 1)
                    piece = 0
                    for t in range(ST):
                        u = a * ST + t
                        pe.wait_ge(relu_done[u % 2], START + i * ST + u // 2)
                        at = slice(t * P, (t + 1) * P)
                        for j, (l, rr) in enumerate(((iqh, ikh), (iqh, ikl), (iql, ikh))):
                            for k0 in range(0, (t + 1) * P, HALF):
                                k1 = min(k0 + HALF, (t + 1) * P)
                                ins = pe.matmul(slots[u % 2][:, k0:k1], l[:, a, at], rr[:, k0:k1],
                                                start=j == 0, stop=j == 2, skip_group_check=True)
                        ins.then_inc(scored, 1)
                        for _ in range(PIECES[t] if more else 0):
                            project(i * 2 + a + 1, 1 - a, piece)
                            piece += 1

                def body(i, last):
                    score(i, 0, True)
                    score(i, 1, not last)
                for piece in range(2 * DT):
                    project(0, 0, piece)
                pairs(pe, body)

            @block.scalar
            def _(act):
                def split_w(j, a):
                    act.wait_ge(raw_in[a], START + j * 64 + 64)
                    act.copy(wh[:, a], w[:, a]).then_inc(wh_done, 1)

                def split_iq(n, a):
                    act.wait_ge(projected, START + n + 1)
                    act.copy(iqh[:, a], ps_iq).then_inc(iqh_done, 1)

                def relus(i, a, more, last):
                    act.wait_ge(wc_done, START + i * 2 + a + 1)
                    for t in range(ST):
                        if t == SPLIT_AT:
                            if more:
                                split_iq(i * 2 + a + 1, 1 - a)
                            if not last:
                                split_w(i + 1, a)
                        u = a * ST + t
                        act.wait_ge(scored, START + i * 2 * ST + u + 1)
                        act.wait_ge(added[u % 2], START + i * ST + u // 2)
                        W = (t + 1) * P
                        act.activation(r[:, u % 2, 0:W], slots[u % 2][:, 0:W], ACT.Relu,
                                       scale=awc[:, a, t:t + 1]).then_inc(relu_done[u % 2], 1)

                def body(i, last):
                    relus(i, 0, True, last)
                    relus(i, 1, not last, last)
                split_w(0, 0)
                split_w(0, 1)
                split_iq(0, 0)
                pairs(act, body)

            @block.vector
            def _(dve):
                def split_iq(n, a):
                    dve.wait_ge(iqh_done, START + n + 1)
                    dve.tensor_tensor(iql[:, a], ps_iq, f32(iqh[:, a]), ALU.subtract).then_inc(iql_done, 1)

                def pick_w(n, a):
                    dve.tensor_copy(awc[:, a, :], aw[:, :, bass.ds(n, 1)].rearrange("p t o -> p (t o)"))
                    dve.tensor_copy(sgc[:, a, :], sg[:, :, bass.ds(n, 1)].rearrange("p t o -> p (t o)")).then_inc(
                        wc_done, 1)

                def adds(i, a, more):
                    dve.wait_ge(wc_done, START + i * 2 + a + 1)
                    for t in range(ST):
                        if t == SPLIT_AT and more:
                            split_iq(i * 2 + a + 1, 1 - a)
                            pick_w(i * 2 + a + 1, 1 - a)
                        u = a * ST + t
                        dve.wait_ge(relu_done[u % 2], START + i * ST + u // 2 + 1)
                        W = (t + 1) * P
                        acc = idx[:, MASK_OFF[t]:MASK_OFF[t] + W]
                        dve.scalar_tensor_tensor(out=acc, in0=r[:, u % 2, 0:W], scalar=sgc[:, a, t:t + 1], in1=acc,
                                                 op0=ALU.mult, op1=ALU.add).then_inc(added[u % 2], 1)

                def body(i, last):
                    adds(i, 0, True)
                    adds(i, 1, not last)
                dve.memset(idx[:, :], 0.0).then_inc(added_zero, 1)
                dve.wait_ge(added_zero, START + 1)
                split_iq(0, 0)
                dve.tensor_copy(awc[:, 0, :], aw[:, :, 0])
                dve.tensor_copy(sgc[:, 0, :], sg[:, :, 0]).then_inc(wc_done, 1)
                pairs(dve, body)
        c.finish()


def ffn(nc, tag, ps, xnh, xnl, x, F, w1_d, w3_d, w2_d, b1_d, b2_d, out_d=None, beside=None):
    gated = w3_d is not None
    NW = 2 if gated else 1
    NC = -(-F // P)
    size = [min(P, F - P * k) for k in range(NC)]
    LOOPS = (NC - 2) // 2
    with ExitStack() as st:
        c = Ctx(nc, st)
        w1 = c.sb(tag + "_w1", [P, 2, NW, DT, P])
        w1h = c.sb(tag + "_w1h", [P, 2, NW, DT, P], F32R)
        w1l = c.sb(tag + "_w1l", [P, 2, NW, DT, P], F32R)
        w2 = c.sb(tag + "_w2", [P, 2, D])
        w2h = c.sb(tag + "_w2h", [P, 2, D], F32R)
        w2l = c.sb(tag + "_w2l", [P, 2, D], F32R)
        g = c.sb(tag + "_g", [P, 2, HALF])
        g1 = c.sb(tag + "_g1", [P, 2, NW, HALF])
        gh = c.sb(tag + "_gh", [P, 2, HALF], F32R)
        gl = c.sb(tag + "_gl", [P, 2, HALF], F32R)
        y = c.sb(tag + "_y", [P, 4, D])
        ones = c.sb(tag + "_ones", [1, P])
        b2 = c.sb(tag + "_b2", [1, D])
        b1 = c.sb(tag + "_b1", [P, NC])
        b2_seen = c.sb(tag + "_b2_seen", [1, 1])
        names = ("b_in", "b_done", "seeded", "out_done", "x_done", "stored")
        b_in, b_done, seeded, out_done, x_done, stored = (c.sem(f"{tag}_{n}") for n in names)
        (w1_in, w2_in, w1h_done, w1l_done, w2h_done, w2l_done, hidden, act_done, g_done, gh_done, gl_done, used) = (
            c.sems(f"{tag}_{n}_", 2) for n in ("w1_in", "w2_in", "w1h_done", "w1l_done", "w2h_done", "w2l_done",
                                               "hidden", "act_done", "g_done", "gh_done", "gl_done", "used"))
        w1_v = [w.rearrange("(k p) n -> p k n", p=P) for w in ((w1_d, w3_d) if gated else (w1_d,))]
        uses = [(NC + 1) // 2, NC // 2]

        def ahead(j, s, by):
            return (j + (s + by) // 2, (s + by) % 2)

        def steps(eng, body):
            with eng.Fori(0, LOOPS) as i:
                for s in range(2):
                    body(i, s, (P, P, P))
            for k in range(2 * LOOPS, NC):
                body(k // 2, k % 2, [size[m] if m < NC else None for m in (k, k + 1, k + 2)])

        c.begin()
        with nc.Block() as block:
            @block.sync
            def _(sp):
                if not gated:
                    sp.dma_start(b2[:, :], b2_d.rearrange("(o n) -> o n", o=1)).then_inc(b_in, 16)
                    sp.dma_start(b1[:, :], b1_d.rearrange("(k p) -> p k", p=P), allow_slow_non_contiguous=True).then_inc(b_in, 16)
                for half in range(2):
                    def body(j, s, sizes):
                        u, n = half * uses[s] + j, sizes[0]
                        at = bass.ds(j * 2 * P + s * P, n)
                        sp.wait_ge(w1l_done[s], START + u)
                        for m in range(NW):
                            sp.dma_start(w1[:, s, m, :, 0:n], w1_v[m][:, :, at]).then_inc(w1_in[s], 16)
                        sp.wait_ge(w2l_done[s], START + u)
                        sp.dma_start(w2[0:n, s], w2_d[at, :]).then_inc(w2_in[s], 16)
                    steps(sp, body)
                if out_d is not None:
                    for half in range(2):
                        sp.wait_ge(x_done, START + half + 1)
                        sp.dma_start(out_d.rearrange("(t p) n -> p t n", p=P)[:, 4 * half:4 * half + 4],
                                     x[:, 4 * half:4 * half + 4]).then_inc(stored, 16)
                    sp.wait_ge(stored, START + 32)

            @block.tensor
            def _(pe):
                for half in range(2):
                    tok = slice(half * HALF, (half + 1) * HALF)

                    def up(j, s, n):
                        u = half * uses[s] + j
                        pe.wait_ge(w1l_done[s], START + u + 1)
                        pe.wait_ge(act_done[s], START + u)
                        for m in range(NW):
                            for k in range(DT):
                                ins = mm3(pe, ps[0:n, 4 + NW * s + m, :], (w1h[:, s, m, k, 0:n], w1l[:, s, m, k, 0:n]),
                                          (xnh[:, k, tok], xnl[:, k, tok]), k == 0, k == DT - 1)
                        ins.then_inc(hidden[s], 1)

                    def down(j, s, n):
                        u = half * uses[s] + j
                        pe.wait_ge(w2l_done[s], START + u + 1)
                        pe.wait_ge(gl_done[s], START + u + 1)
                        for t in range(4):
                            at = slice(t * P, (t + 1) * P)
                            ins = mm3(pe, ps[:, t, :], (gh[0:n, s, at], gl[0:n, s, at]), (w2h[0:n, s], w2l[0:n, s]),
                                      False, True)
                        ins.then_inc(used[s], 1)

                    def body(j, s, sizes):
                        if sizes[1] is not None:
                            up(*ahead(j, s, 1), sizes[1])
                        down(j, s, sizes[0])

                    up(0, 0, size[0])
                    pe.wait_ge(b_done, START + 2)
                    pe.wait_ge(out_done, START + half)
                    for t in range(4):
                        pe.matmul(ps[:, t, :], ones[:, :], b2[:, :], start=True, stop=False, skip_group_check=True)
                    steps(pe, body)

            @block.scalar
            def _(act):
                for half in range(2):
                    def split_w1(j, s, n):
                        u = half * uses[s] + j
                        act.wait_ge(w1_in[s], START + (u + 1) * 16 * NW)
                        act.wait_ge(hidden[s], START + u)
                        act.copy(w1h[:, s, :, :, 0:n], w1[:, s, :, :, 0:n]).then_inc(w1h_done[s], 1)

                    def split_w2(j, s, n):
                        u = half * uses[s] + j
                        act.wait_ge(w2_in[s], START + (u + 1) * 16)
                        act.wait_ge(used[s], START + u)
                        act.copy(w2h[0:n, s], w2[0:n, s]).then_inc(w2h_done[s], 1)

                    def activate(j, s, n):
                        u = half * uses[s] + j
                        act.wait_ge(hidden[s], START + u + 1)
                        if gated:
                            act.wait_ge(g_done[s], START + u)
                            act.activation(g1[0:n, s, 0], ps[0:n, 4 + 2 * s, :], ACT.Silu)
                            act.copy(g1[0:n, s, 1], ps[0:n, 5 + 2 * s, :]).then_inc(act_done[s], 1)
                            act.wait_ge(g_done[s], START + u + 1)
                        else:
                            act.wait_ge(gl_done[s], START + u)
                            bias = b1[0:n, bass.ds(j * 2 + s, 1)]
                            act.activation(g[0:n, s], ps[0:n, 4 + s, :], ACT.Gelu_apprx_tanh, bias=bias).then_inc(
                                act_done[s], 1)
                            act.wait_ge(act_done[s], START + u + 1)
                        act.wait_ge(used[s], START + u)
                        act.copy(gh[0:n, s], g[0:n, s]).then_inc(gh_done[s], 1)

                    def body(j, s, sizes):
                        if sizes[2] is not None:
                            split_w1(*ahead(j, s, 2), sizes[2])
                        if sizes[1] is not None:
                            split_w2(*ahead(j, s, 1), sizes[1])
                            activate(*ahead(j, s, 1), sizes[1])

                    if half == 0 and not gated:
                        act.wait_ge(b_in, START + 32)
                    split_w1(0, 0, P)
                    split_w1(0, 1, P)
                    split_w2(0, 0, P)
                    activate(0, 0, P)
                    steps(act, body)
                    for s in range(2):
                        act.wait_ge(used[s], START + (half + 1) * uses[s])
                    act.wait_ge(x_done, START + half)
                    act.copy(y[:, :, :], ps[:, 0:4, :]).then_inc(out_done, 1)

            @block.gpsimd
            def _(pool):
                pool.memset(ones[:, :], 1.0).then_inc(b_done, 1)
                if gated:
                    pool.memset(b2[:, :], 0.0).then_inc(b_done, 1)
                else:
                    pool.wait_ge(b_in, START + 32)
                    pool.memset(b2_seen[:, :], 0.0).then_inc(b_done, 1)
                for half in range(2):
                    def split_w1(j, s, n):
                        u = half * uses[s] + j
                        pool.wait_ge(w1h_done[s], START + u + 1)
                        for m in range(NW):
                            ins = pool.tensor_tensor(w1l[:, s, m, :, 0:n], w1[:, s, m, :, 0:n],
                                                     f32(w1h[:, s, m, :, 0:n]), ALU.subtract)
                        ins.then_inc(w1l_done[s], 1)

                    def split_w2(j, s, n):
                        u = half * uses[s] + j
                        pool.wait_ge(w2h_done[s], START + u + 1)
                        pool.tensor_tensor(w2l[0:n, s], w2[0:n, s], f32(w2h[0:n, s]), ALU.subtract).then_inc(
                            w2l_done[s], 1)

                    def split_g(j, s, n):
                        u = half * uses[s] + j
                        if gated:
                            pool.wait_ge(act_done[s], START + u + 1)
                            pool.wait_ge(gl_done[s], START + u)
                            pool.tensor_tensor(g[0:n, s], g1[0:n, s, 0], g1[0:n, s, 1], ALU.mult).then_inc(g_done[s], 1)
                        pool.wait_ge(gh_done[s], START + u + 1)
                        pool.tensor_tensor(gl[0:n, s], g[0:n, s], f32(gh[0:n, s]), ALU.subtract).then_inc(gl_done[s], 1)

                    def body(j, s, sizes):
                        if sizes[2] is not None:
                            split_w1(*ahead(j, s, 2), sizes[2])
                        if sizes[1] is not None:
                            split_w2(*ahead(j, s, 1), sizes[1])
                            split_g(*ahead(j, s, 1), sizes[1])

                    split_w1(0, 0, P)
                    split_w1(0, 1, P)
                    split_w2(0, 0, P)
                    split_g(0, 0, P)
                    steps(pool, body)
                    pool.wait_ge(out_done, START + half + 1)
                    mine = x[:, 4 * half:4 * half + 4]
                    pool.tensor_tensor(mine, mine, y[:, :, :], ALU.add).then_inc(x_done, 1)

            if beside is not None:
                @block.vector
                def _(dve):
                    beside(dve)
        c.finish()


def attention(nc, tag, ps, IT, HP, passes, mask_of, scale, vst, qwork, ctx_d, peel):
    NU = HP * ST
    AHEAD = 7
    NT = 3
    CPH = 12
    layer0 = qwork["layer0"]
    with ExitStack() as st:
        c = Ctx(nc, st)
        sm = [c.sb(f"{tag}_sm{k}", [P, (S, HALF)[k]]) for k in range(2)]
        p = [c.sb(f"{tag}_p{k}", [P, 2, (S, HALF)[k]]) for k in range(2)]
        nmax = c.sb(tag + "_nmax", [P, 4])
        rsum = c.sb(tag + "_rsum", [P, 4])
        rinv = c.sb(tag + "_rinv", [P, 4])
        pth = [c.sb(f"{tag}_pth{g}", [P, 4 * g + 4, HALF], F32R) for g in range(2)]
        ptl = [c.sb(f"{tag}_ptl{g}", [P, 4 * g + 4, HALF], F32R) for g in range(2)]
        ctxst = c.sb(tag + "_ctxst", [P, S])
        (scored, max_done, exp_done, inv_done, norm_done, turned, hi_done, ctx_done) = (
            c.sem(f"{tag}_{n}") for n in ("scored", "max_done", "exp_done", "inv_done", "norm_done", "turned",
                                          "hi_done", "ctx_done"))
        passed, stored = c.sem(tag + "_passed"), c.sem(tag + "_sp_passed")
        lo_done = c.sems(tag + "_lo_done", NT)
        pv_done, ctx_out = c.sem(tag + "_pv_done"), c.sem(tag + "_ctx_out")
        slots = [ps[:, 0:2, :].rearrange("p b n -> p (b n)"), ps[:, 2, :]]
        bank_t = (3, 4, 5)
        banks_c = (6,) if layer0 else (6, 7)
        results = [ps[:, b, 0:PAIR] for b in banks_c]
        parts = [(1, 4), (2, 2), (5, 6), (6, 0)]
        sems = dict(scored=scored, ctx_done=ctx_done, pv_done=pv_done)

        def unit(v):
            a, r = divmod(v, ST)
            t = 4 + r // 2 if r % 2 == 0 else 3 - r // 2
            return a, t, r % 2, (t + 1) * P

        def chunks_of(v):
            r = v % ST
            t = unit(v % NU)[1]
            if r % 2 == 0:
                return [(3 * (r // 2), 0, 4), (3 * (r // 2) + 1, 4, t - 3)]
            return [(3 * (r // 2) + 2, 0, t + 1)]

        def run(eng, step):
            def body(i, left):
                for u in range(NU):
                    step(i, u, left)
            for u in range(-AHEAD, 0):
                step(0, u, IT)
            with eng.Fori(0, IT - peel) as i:
                body(i, peel)
            for left in reversed(range(peel)):
                body(IT - 1 - left, left)

        def there(v, left):
            return v >= 0 and (v < NU or left > 0)

        q = qwork["make"](c, sems)

        c.begin()
        with nc.Block() as block:
            @block.tensor
            def _(pe):
                def scores(i, v):
                    a, t, kind, w = unit(v % NU)
                    q["ready"](pe, i, v)
                    if v >= 2:
                        pe.wait_ge(max_done, START + i * NU + v - 1)
                    at = slice(t * P, (t + 1) * P)
                    lr = passes(i, v // NU, a)
                    for j, (l, r) in enumerate(lr):
                        for k0 in range(0, w, HALF):
                            k1 = min(k0 + HALF, w)
                            ins = pe.matmul(slots[kind][:, k0:k1], l(at), r(k0, k1), start=j == 0,
                                            stop=j == len(lr) - 1, skip_group_check=True)
                    ins.then_inc(scored, 1)

                def turn(i, v):
                    _, t, kind, w = unit(v % NU)
                    pe.wait_ge(norm_done, START + i * NU + v + 1)
                    for n, j0, m in chunks_of(v):
                        if v >= 2:
                            pe.wait_ge(lo_done[n % NT], START + (i * HP + v // ST) * (CPH // NT) + n // NT)
                        for k in range(m):
                            ins = pe.transpose(ps[:, bank_t[n % NT], k * P:(k + 1) * P],
                                               p[kind][:, v // 2 % 2, (j0 + k) * P:(j0 + k + 1) * P],
                                               qwork["ident"][:, :])
                        ins.then_inc(turned, 1)

                def weigh(i, a, k, t):
                    g = t // 4
                    last = 2 * (t % 4) + 2 if g else 2 * (3 - t) + 1
                    for n, _, _ in chunks_of(last):
                        pe.wait_ge(lo_done[n % NT], START + (i * HP + a) * (CPH // NT) + n // NT + 1)
                    pe.wait_ge(ctx_done, START + (i * HP + a) * 4 + k + 1)
                    for j in range(t + 2):
                        n0 = PAIR // 2 if j == t + 1 else 0
                        c0 = t % 4 * P
                        for h, pt in enumerate((pth[g], ptl[g])):
                            ins = pe.matmul(results[k % len(banks_c)][:, n0:PAIR], vst(j), pt[:, j, c0 + n0:c0 + PAIR],
                                            start=j == 0 and h == 0, stop=j == t + 1 and h == 1,
                                            skip_group_check=True)
                    ins.then_inc(pv_done, 1)

                def step(i, u, left):
                    if there(u + 7, left):
                        scores(i, u + 7)
                    if there(u + 3, left):
                        turn(i, u + 3)
                    q["pe"](pe, i, u, left)
                    for k, (s, t) in enumerate(parts):
                        if u >= 0 and u % ST == s:
                            q["v_ready"](pe, i, u // ST, k)
                            weigh(i, u // ST, k, t)

                pe.sem_inc(ctx_done, len(banks_c))
                q["pe_first"](pe)
                run(pe, step)

            @block.vector
            def _(dve):
                def maximum(i, v):
                    a, t, kind, w = unit(v % NU)
                    pause(dve, scored, i * NU + v + 1, passed)
                    dve.tensor_tensor_reduce(out=sm[kind][:, 0:w], in0=slots[kind][:, 0:w], in1=mask_of(t),
                                             scale=-scale, scalar=3.0e38, op0=ALU.add, op1=ALU.min,
                                             accum_out=nmax[:, v % 4:v % 4 + 1]).then_inc(max_done, 1)

                def inverse(i, v):
                    k = v % 4
                    dve.wait_ge(exp_done, START + i * NU + v + 1)
                    dve.reciprocal(rinv[:, k:k + 1], rsum[:, k:k + 1]).then_inc(inv_done, 1)

                def low(i, v):
                    _, t, kind, w = unit(v % NU)
                    g = t // 4
                    at = slice((t % 4) * P, (t % 4 + 1) * P)
                    for n, j0, m in chunks_of(v):
                        dve.wait_ge(hi_done, START + (i * HP + v // ST) * CPH + n + 1)
                        dve.tensor_tensor(ptl[g][:, j0:j0 + m, at], bank4(ps, bank_t[n % NT])[:, 0:m],
                                          f32(pth[g][:, j0:j0 + m, at]), ALU.subtract).then_inc(lo_done[n % NT], 1)

                def step(i, u, left):
                    if there(u + 5, left):
                        inverse(i, u + 5)
                    q["dve"](dve, i, u, left)
                    for k, (s, t) in enumerate(parts):
                        if layer0 and u >= 0 and u % ST == s + 1:
                            q["dve_ctx"](dve, i, u // ST, k, results[k % len(banks_c)], ctxst[:, t * P:t * P + PAIR], ctx_out)
                    if there(u + 2, left):
                        low(i, u + 2)
                    if there(u + 7, left):
                        maximum(i, u + 7)

                q["dve_first"](dve)
                run(dve, step)

            @block.scalar
            def _(act):
                def exponential(i, v):
                    a, t, kind, w = unit(v % NU)
                    act.wait_ge(max_done, START + i * NU + v + 1)
                    act.activation(p[kind][:, v // 2 % 2, 0:w], sm[kind][:, 0:w], ACT.Exp,
                                   bias=nmax[:, v % 4:v % 4 + 1], scale=-1.0,
                                   accum_out=rsum[:, v % 4:v % 4 + 1]).then_inc(exp_done, 1)

                def high(i, v):
                    _, t, kind, w = unit(v % NU)
                    g = t // 4
                    at = slice((t % 4) * P, (t % 4 + 1) * P)
                    for n, j0, m in chunks_of(v):
                        act.wait_ge(turned, START + (i * HP + v // ST) * CPH + n + 1)
                        act.copy(pth[g][:, j0:j0 + m, at], bank4(ps, bank_t[n % NT])[:, 0:m]).then_inc(hi_done, 1)

                def step(i, u, left):
                    for k, (s, t) in enumerate(parts):
                        if u >= 0 and u % ST == s + 1:
                            q["act_ctx"](act, i, u // ST, k, results[k % len(banks_c)], ctxst[:, t * P:t * P + PAIR], ctx_out)
                    if there(u + 6, left):
                        exponential(i, u + 6)
                    if there(u + 3, left):
                        high(i, u + 3)
                    q["act"](act, i, u, left)

                q["act_first"](act)
                run(act, step)

            @block.gpsimd
            def _(pool):
                def normalise(i, v):
                    a, t, kind, w = unit(v % NU)
                    pause(pool, inv_done, i * NU + v + 1, passed)
                    mine = p[kind][:, v // 2 % 2, 0:w]
                    pool.tensor_scalar(mine, mine, rinv[:, v % 4:v % 4 + 1], 1.0, ALU.mult, ALU.mult).then_inc(
                        norm_done, 1)

                def step(i, u, left):
                    if there(u + 5, left):
                        normalise(i, u + 5)
                    q["pool"](pool, i, u, left)

                q["pool_first"](pool)
                run(pool, step)

            @block.sync
            def _(sp):
                sp.sem_inc(ctx_out, 1)
                q["sp_first"](sp)

                def body(i, left):
                    q["sp"](sp, i, left)
                    pause(sp, ctx_done, (i + 1) * 4 * HP + len(banks_c), stored)
                    sp.dma_start(ctx_d[i], ctxst[:, :]).then_inc(ctx_out, 16)
                with sp.Fori(0, IT - peel) as i:
                    body(i, peel)
                for left in reversed(range(peel)):
                    body(IT - 1 - left, left)
                sp.wait_ge(ctx_out, START + 16 * IT + 1)
        c.finish()


def latent_queries(nc, ps, ident, xq, wabs_d, cos_d, sin_d, tables):
    qlh, qll = xq
    cosT, sinT = tables
    pieces = [(0, "sw", 0, 0), (1, "sw", 0, 1), (2, "m", 0, 0), (4, "m", 0, 1), (7, "m", 1, 0), (10, "m", 1, 1)]
    NPC = len(pieces)
    W_STEP = 12
    bank_q = 7
    q = {"layer0": True, "ident": ident}

    def make(c, sems):
        wraw = c.sb("lq_wraw", [QC, 2, 3, P])
        wh = c.sb("lq_wh", [QC, 2, 3, P], F32R)
        wl = c.sb("lq_wl", [QC, 2, 3, P], F32R)
        t1 = c.sb("lq_t1", [P, 2, HALF])
        t2 = c.sb("lq_t2", [P, 2, S])
        qh = c.sb("lq_qh", [P, 2, S], F32R)
        ql = c.sb("lq_ql", [P, 2, S], F32R)
        tmp = c.sb("lq_tmp", [KVR, 2, PAIR])
        raw_in, tab_in, wh_done, wl_done, q_mm, q_evac, add_done, qh_done, q_lo_done, tmp_done = (
            c.sem("lq_" + n) for n in ("raw_in", "tab_in", "wh_done", "wl_done", "q_mm", "q_evac", "add_done",
                                       "qh_done", "q_lo_done", "tmp_done"))
        scored, ctx_done, pv_done = sems["scored"], sems["ctx_done"], sems["pv_done"]
        q["bufs"] = (qh, ql)

        def ready(pe, i, v):
            if v % ST == 0:
                pe.wait_ge(q_lo_done, START + i * 4 + 2 * (v // ST) + 2)

        def piece(pair, k):
            return pair * NPC + k, pair * 4 + k - 2

        def of_step(u, left):
            return [k for k, (s, _, _, _) in enumerate(pieces) if s == u and left > 0]

        def pe_piece(pe, pair, k):
            _, kind, a, g = pieces[k]
            K, M = piece(pair, k)
            pe.wait_ge(wl_done, START + pair + 1)
            pe.wait_ge(q_evac, START + K)
            b = a if kind == "m" else 2
            at = slice(g * HALF, (g + 1) * HALF)
            for h in range(2):
                ins = mm3(pe, ps[:, bank_q, :], (wh[:, h, b], wl[:, h, b]), (qlh[:, h, at], qll[:, h, at]),
                          h == 0, h == 1)
            ins.then_inc(q_mm, 1)

        def dve_piece(dve, pair, k, first=False):
            _, kind, a, g = pieces[k]
            K, M = piece(pair, k)
            dve.wait_ge(q_mm, START + K + 1)
            at = slice(g * HALF, (g + 1) * HALF)
            if kind == "sw":
                if not first:
                    dve.wait_ge(add_done, START + pair * 4)
                for h in range(2):
                    rows = slice(64 * h, 64 * h + 64)
                    ins = dve.tensor_tensor(t2[64:P, h, at], ps[rows, bank_q, :], sinT[rows, at], ALU.mult)
            else:
                if not first or k >= 4:
                    dve.wait_ge(q_lo_done, START + M - 1)
                ins = dve.tensor_tensor(t1[:, g], ps[:, bank_q, :], cosT[:, at], ALU.mult)
            ins.then_inc(q_evac, 1)

        def pool_add(pool, pair, k):
            _, kind, a, g = pieces[k]
            pool.wait_ge(q_evac, START + piece(pair, k)[0] + 1)
            pool.tensor_tensor(t1[:, g], t1[:, g], t2[:, a, g * HALF:(g + 1) * HALF], ALU.add).then_inc(add_done, 1)

        def act_high(act, pair, k, first=False):
            _, kind, a, g = pieces[k]
            act.wait_ge(add_done, START + piece(pair, k)[1] + 1)
            if not first:
                act.wait_ge(scored, START + (pair - 1) * 2 * ST + (a + 1) * ST)
            act.copy(qh[:, a, g * HALF:(g + 1) * HALF], t1[:, g]).then_inc(qh_done, 1)

        def pool_low(pool, pair, k):
            _, kind, a, g = pieces[k]
            pool.wait_ge(qh_done, START + piece(pair, k)[1] + 1)
            at = slice(g * HALF, (g + 1) * HALF)
            pool.tensor_tensor(ql[:, a, at], t1[:, g], f32(qh[:, a, at]), ALU.subtract).then_inc(q_lo_done, 1)

        def act_weights(act, pair, first=False):
            act.wait_ge(raw_in, START + pair * 16 + 16)
            if not first:
                act.wait_ge(q_mm, START + pair * NPC)
            act.copy(wh[:, :, :, :], wraw[:, :, :, :]).then_inc(wh_done, 1)

        def pool_weights(pool, pair):
            pool.wait_ge(wh_done, START + pair + 1)
            pool.tensor_tensor(wl[:, :, :, :], wraw[:, :, :, :], f32(wh[:, :, :, :]), ALU.subtract).then_inc(wl_done, 1)

        def load_weights(sp, pair):
            sp.dma_start(wraw[:, :, :, :].rearrange("p c b n -> p (c b n)"), wabs_d[pair]).then_inc(raw_in, 16)

        def pe_first(pe):
            for k in range(NPC):
                if k:
                    pe_piece(pe, 0, k)
                else:
                    pe.wait_ge(wl_done, START + 1)
                    for h in range(2):
                        ins = mm3(pe, ps[:, bank_q, :], (wh[:, h, 2], wl[:, h, 2]), (qlh[:, h, 0:HALF], qll[:, h, 0:HALF]),
                                  h == 0, h == 1)
                    ins.then_inc(q_mm, 1)

        def dve_first(dve):
            dve.memset(t2[0:64, :, :], 0.0)
            dve.wait_ge(tab_in, START + 32)
            for k in range(NPC):
                dve_piece(dve, 0, k, first=True)

        def act_first(act):
            act_weights(act, 0, first=True)
            for k in range(2, NPC):
                act_high(act, 0, k, first=True)
            act_weights(act, 1)

        def pool_first(pool):
            pool_weights(pool, 0)
            for k in range(2, NPC):
                pool_add(pool, 0, k)
                pool_low(pool, 0, k)
            pool_weights(pool, 1)

        def sp_first(sp):
            load_weights(sp, 0)
            sp.dma_start(cosT[:, :], cos_d).then_inc(tab_in, 16)
            sp.dma_start(sinT[:, :], sin_d).then_inc(tab_in, 16)
            sp.wait_ge(wl_done, START + 1)
            load_weights(sp, 1)

        def pe_hook(pe, i, u, left):
            for k in of_step(u, left):
                pe_piece(pe, i + 1, k)

        def dve_hook(dve, i, u, left):
            for k in of_step(u - 1, left):
                dve_piece(dve, i + 1, k)

        def act_hook(act, i, u, left):
            for k in of_step(u - 2, left):
                if k >= 2:
                    act_high(act, i + 1, k)
            if u == W_STEP and left > 1:
                act_weights(act, i + 2)

        def pool_hook(pool, i, u, left):
            for k in of_step(u - 3, left):
                if k >= 2:
                    pool_low(pool, i + 1, k)
            for k in of_step(u - 1, left):
                if k >= 2:
                    pool_add(pool, i + 1, k)
            if u == W_STEP + 1 and left > 1:
                pool_weights(pool, i + 2)

        def sp_hook(sp, i, left):
            if left > 1:
                sp.wait_ge(wl_done, START + i + 2)
                load_weights(sp, i + 2)

        def act_ctx(act, i, a, k, result, out, ctx_out):
            act.wait_ge(pv_done, START + (i * 2 + a) * 4 + k + 1)
            act.copy(tmp[:, k % 2], result[KVR:2 * KVR, :]).then_inc(tmp_done, 1)

        def dve_ctx(dve, i, a, k, result, out, ctx_out):
            dve.wait_ge(tmp_done, START + (i * 2 + a) * 4 + k + 1)
            if a == 0 and k == 0:
                dve.wait_ge(ctx_out, START + i * 16 + 1)
            dve.tensor_tensor(out[64 * a:64 * a + 64, :], result[0:KVR, :], tmp[:, k % 2], ALU.add).then_inc(ctx_done, 1)

        q.update(ready=ready, pe=pe_hook, dve=dve_hook, act=act_hook, pool=pool_hook, sp=sp_hook, pe_first=pe_first,
                 dve_first=dve_first, act_first=act_first, pool_first=pool_first, sp_first=sp_first, act_ctx=act_ctx,
                 dve_ctx=dve_ctx, v_ready=lambda *_: None)
        return q

    q["make"] = make
    return q


def stacked_queries(nc, ps, ident, vs_all, vg, qd, kvd):
    q = {"layer0": False, "ident": ident}
    q_v = qd.rearrange("l (i a p) t -> l i a p t", a=REP1, p=HD1)
    k_v = kvd.rearrange("l (g e p) t -> l e p g t", e=2, p=HD1)

    def make(c, sems):
        qst = c.sb("sq_qst", [P, REP1, S], F32R)
        kst = c.sb("sq_kst", [P, G1, S], F32R)
        zeroed, k_in, vg_done = c.sem("sq_zeroed"), c.sem("sq_k_in"), c.sem("sq_vg_done")
        q_in = c.sems("sq_q_in", REP1)
        scored, ctx_done, pv_done = sems["scored"], sems["ctx_done"], sems["pv_done"]
        q["bufs"] = (qst, kst)

        def load_q(sp, i, a):
            for b in range(4):
                sp.dma_start(f32(qst[b * HD1:(b + 1) * HD1, a]), q_v[b // 2][i][a]).then_inc(q_in[a], 16)

        def ready(pe, i, v):
            if v % ST == 0:
                a = (v // ST) % REP1
                pe.wait_ge(q_in[a], START + (i + v // (REP1 * ST)) * 64 + 64)

        def sp_first(sp):
            for a in range(REP1):
                load_q(sp, 0, a)
            for b in range(4):
                sp.dma_start(f32(kst[b * HD1:(b + 1) * HD1, :, :]), k_v[b % 2][0]).then_inc(k_in, 16)

        def sp_hook(sp, i, left):
            if left:
                for a in range(REP1):
                    sp.wait_ge(scored, START + i * REP1 * ST + (a + 1) * ST)
                    load_q(sp, i + 1, a)

        def dve_first(dve):
            dve.memset(f32(qst[64:P, :, :]), 0.0).then_inc(zeroed, 1)
            dve.memset(f32(kst[64:P, :, :]), 0.0).then_inc(zeroed, 1)

        def pe_first(pe):
            pe.wait_ge(zeroed, START + 2)
            pe.wait_ge(k_in, START + 64)

        def copy_values(act, i, first=False):
            if not first:
                act.wait_ge(pv_done, START + i * REP1 * 4)
            src = vs_all[:, :, bass.ds(i, 1), :].broadcast_to([P, ST, REP1, 2 * HD1])
            act.copy(vg[:, :, :, :], src).then_inc(vg_done, 1)

        def act_first(act):
            copy_values(act, 0, first=True)

        def act_hook(act, i, u, left):
            if u == REP1 * ST - 1 and left:
                copy_values(act, i + 1)

        def v_ready(pe, i, a, k):
            if a == 0 and k == 0:
                pe.wait_ge(vg_done, START + i + 1)

        def act_ctx(act, i, a, k, result, out, ctx_out):
            act.wait_ge(pv_done, START + (i * REP1 + a) * 4 + k + 1)
            if a == 0 and k == 0:
                act.wait_ge(ctx_out, START + i * 16 + 1)
            rows = slice(32 * a, 32 * a + 32)
            act.copy(out[rows, :], result[rows, :]).then_inc(ctx_done, 1)

        def none(*_):
            pass

        q.update(ready=ready, pe=none, dve=none, act=act_hook, pool=none, sp=sp_hook, pe_first=pe_first,
                 dve_first=dve_first, act_first=act_first, pool_first=none, sp_first=sp_first, act_ctx=act_ctx,
                 v_ready=v_ready)
        return q

    q["make"] = make
    return q


def project_out(nc, tag, ps, x, NK, ctx_d, load_w, w_dmas, bias_d):
    NS = 4
    with ExitStack() as st:
        c = Ctx(nc, st)
        cr = c.sb(tag + "_cr", [P, NS, HALF])
        ch = c.sb(tag + "_ch", [P, NS, HALF], F32R)
        cl = c.sb(tag + "_cl", [P, NS, HALF], F32R)
        wr = c.sb(tag + "_wr", [P, NS, D])
        wh = c.sb(tag + "_wh", [P, NS, D], F32R)
        wl = c.sb(tag + "_wl", [P, NS, D], F32R)
        ones = c.sb(tag + "_ones", [1, P])
        b = c.sb(tag + "_b", [1, D])
        b_in, b_done, summed, x_done = (c.sem(f"{tag}_{n}") for n in ("b_in", "b_done", "summed", "x_done"))
        raw_in, hi_done, cl_done, wl_done, used = (
            c.sems(f"{tag}_{n}_", NS) for n in ("raw_in", "hi_done", "cl_done", "wl_done", "used"))
        NJ = NK // NS

        def tiles(eng, half, body):
            with eng.Fori(0, NJ) as i:
                for s in range(NS):
                    body(i * NS + s, s, i + half * NJ)

        c.begin()
        with nc.Block() as block:
            @block.sync
            def _(sp):
                if bias_d is not None:
                    sp.dma_start(b[:, :], bias_d.rearrange("(o n) -> o n", o=1)).then_inc(b_in, 16)
                for half in range(2):
                    def body(k, s, u):
                        sp.wait_ge(cl_done[s], START + u)
                        sp.wait_ge(wl_done[s], START + u)
                        sp.dma_start(cr[:, s], ctx_d[k][:, half * HALF:(half + 1) * HALF]).then_inc(raw_in[s], 16)
                        load_w(sp, k, wr[:, s], raw_in[s])
                    tiles(sp, half, body)

            @block.scalar
            def _(act):
                for half in range(2):
                    def body(k, s, u):
                        act.wait_ge(raw_in[s], START + (u + 1) * 16 * (1 + w_dmas))
                        act.wait_ge(used[s], START + u)
                        act.copy(ch[:, s], cr[:, s])
                        act.copy(wh[:, s], wr[:, s]).then_inc(hi_done[s], 1)
                    tiles(act, half, body)

            @block.gpsimd
            def _(pool):
                pool.memset(ones[:, :], 1.0).then_inc(b_done, 1)
                if bias_d is None:
                    pool.memset(b[:, :], 0.0).then_inc(b_done, 1)
                for half in range(2):
                    def body(k, s, u):
                        pool.wait_ge(hi_done[s], START + u + 1)
                        pool.tensor_tensor(wl[:, s], wr[:, s], f32(wh[:, s]), ALU.subtract).then_inc(wl_done[s], 1)
                    tiles(pool, half, body)

            @block.tensor
            def _(pe):
                pe.wait_ge(b_done, START + (1 if bias_d is not None else 2))
                if bias_d is not None:
                    pe.wait_ge(b_in, START + 16)
                for half in range(2):
                    for t in range(4):
                        pe.matmul(ps[:, 4 * half + t, :], ones[:, :], b[:, :], start=True, stop=False,
                                  skip_group_check=True)

                    def body(k, s, u):
                        pe.wait_ge(cl_done[s], START + u + 1)
                        pe.wait_ge(wl_done[s], START + u + 1)
                        for t in range(4):
                            at = slice(t * P, (t + 1) * P)
                            ins = mm3(pe, ps[:, 4 * half + t, :], (ch[:, s, at], cl[:, s, at]), (wh[:, s], wl[:, s]),
                                      False, True)
                        ins.then_inc(used[s], 1)
                    tiles(pe, half, body)

            @block.vector
            def _(dve):
                for half in range(2):
                    def body(k, s, u):
                        dve.wait_ge(hi_done[s], START + u + 1)
                        dve.tensor_tensor(cl[:, s], cr[:, s], f32(ch[:, s]), ALU.subtract).then_inc(cl_done[s], 1)
                    tiles(dve, half, body)
                    for s in range(NS):
                        dve.wait_ge(used[s], START + (half + 1) * NJ)
                    mine = x[:, 4 * half:4 * half + 4]
                    dve.tensor_tensor(mine, ps[:, 4 * half:4 * half + 4, :], mine, ALU.add).then_inc(x_done, 1)
        c.finish()


def layer1_qkv(nc, ps, xnh, xnl, wq, wkv, qd, kvd, vs_all):
    NQ, NKV = D // P, 2 * G1 * HD1 // P
    with ExitStack() as st:
        c = Ctx(nc, st)
        NW = D + 2 * G1 * HD1
        w = c.sb("qk_w", [P, DT, NW])
        wh = c.sb("qk_wh", [P, DT, NW], F32R)
        wl = c.sb("qk_wl", [P, DT, NW], F32R)
        oh = c.sb("qk_oh", [P, NQ + NKV, S], F32R)
        ol = c.sb("qk_ol", [P, NQ + NKV, S], F32R)
        w_in, wh_done, wl_done, done, hi_done, lo_done, stored = (
            c.sem("qk_" + n) for n in ("w_in", "wh_done", "wl_done", "done", "hi_done", "lo_done", "stored"))
        tasks = [("T", m, h) for m in range(NQ + NKV) for h in range(2)] + [("V", t, 0) for t in range(ST)]
        c.begin()
        with nc.Block() as block:
            @block.sync
            def _(sp):
                sp.dma_start(w[:, :, 0:D], wq.rearrange("(k p) n -> p k n", p=P)).then_inc(w_in, 16)
                sp.dma_start(w[:, :, D:], wkv.rearrange("(k p) n -> p k n", p=P)).then_inc(w_in, 16)
                for m in range(NQ + NKV):
                    sp.wait_ge(lo_done, START + 2 * m + 2)
                    for l, o in enumerate((oh, ol)):
                        dst = qd[l][m * P:(m + 1) * P, :] if m < NQ else kvd[l][(m - NQ) * P:(m - NQ + 1) * P, :]
                        sp.dma_start(dst, f32(o[:, m])).then_inc(stored, 16)
                sp.wait_ge(stored, START + 32 * (NQ + NKV))

            @block.gpsimd
            def _(pool):
                for m in range(0, NQ + NKV, 2):
                    pool.wait_ge(wh_done, START + m + 2)
                    at = slice((m + 1) * P, (m + 2) * P)
                    pool.tensor_tensor(wl[:, :, at], w[:, :, at], f32(wh[:, :, at]), ALU.subtract).then_inc(wl_done, 1)

            @block.scalar
            def _(act):
                act.wait_ge(w_in, START + 32)
                for m in range(NQ + NKV):
                    at = slice(m * P, (m + 1) * P)
                    act.copy(wh[:, :, at], w[:, :, at]).then_inc(wh_done, 1)
                for n, (kind, m, h) in enumerate(tasks):
                    act.wait_ge(done, START + n + 1)
                    if kind == "T":
                        act.copy(oh[:, m, h * HALF:(h + 1) * HALF], ps[:, n % 8, :]).then_inc(hi_done, 1)
                    else:
                        v = ps[:, n % 8, 0:2 * G1 * HD1].rearrange("p (g e n) -> p g e n", e=2, n=HD1)[:, :, 1, :]
                        act.copy(vs_all[:, m, :, 0:HD1], v).then_inc(hi_done, 1)

            @block.vector
            def _(dve):
                for m in range(0, NQ + NKV, 2):
                    dve.wait_ge(wh_done, START + m + 1)
                    at = slice(m * P, (m + 1) * P)
                    dve.tensor_tensor(wl[:, :, at], w[:, :, at], f32(wh[:, :, at]), ALU.subtract).then_inc(wl_done, 1)
                for n, (kind, m, h) in enumerate(tasks):
                    dve.wait_ge(hi_done, START + n + 1)
                    if kind == "T":
                        at = slice(h * HALF, (h + 1) * HALF)
                        dve.tensor_tensor(ol[:, m, at], ps[:, n % 8, :], f32(oh[:, m, at]), ALU.subtract).then_inc(lo_done, 1)
                    else:
                        v = ps[:, n % 8, 0:2 * G1 * HD1].rearrange("p (g e n) -> p g e n", e=2, n=HD1)[:, :, 1, :]
                        dve.tensor_tensor(vs_all[:, m, :, HD1:], v, f32(vs_all[:, m, :, 0:HD1]), ALU.subtract).then_inc(
                            lo_done, 1)

            @block.tensor
            def _(pe):
                pe.wait_ge(wl_done, START + NQ + NKV)
                for n, (kind, m, h) in enumerate(tasks):
                    if n >= 8:
                        pe.wait_ge(lo_done, START + n - 7)
                    for k in range(DT):
                        if kind == "T":
                            a1, a2 = slice(m * P, (m + 1) * P), slice(h * HALF, (h + 1) * HALF)
                            ins = mm3(pe, ps[:, n % 8, :], (wh[:, k, a1], wl[:, k, a1]), (xnh[:, k, a2], xnl[:, k, a2]),
                                      k == 0, k == DT - 1)
                        else:
                            a1 = slice(m * P, (m + 1) * P)
                            ins = mm3(pe, ps[:, n % 8, 0:2 * G1 * HD1], (xnh[:, k, a1], xnl[:, k, a1]),
                                      (wh[:, k, D:], wl[:, k, D:]), k == 0, k == DT - 1)
                    ins.then_inc(done, 1)
        c.finish()


def top_keys(dve, c_sem, idx, maskb, strip):
    n = 0

    def step(ins):
        nonlocal n
        n += 1
        ins.then_inc(c_sem[0], 1)
        dve.wait_ge(c_sem[0], START + n)

    top8 = c_sem[1]
    ROUNDS = TOPK // 8
    dve.tensor_copy(maskb[:, 0:P], strip[:, S - P:]).then_inc(c_sem[0], 1)
    n += 1
    for t in range(1, ST):
        row = idx[:, MASK_OFF[t]:MASK_OFF[t + 1]]
        diag = idx[:, MASK_OFF[t] + t * P:MASK_OFF[t + 1]]
        step(dve.tensor_tensor(diag, diag, strip[:, S - P:], ALU.add))
        with dve.Fori(0, ROUNDS // 4) as r:
            for k in range(1, 9, 2):
                dve.max(top8[:, :], row).then_inc(c_sem[0], 1)
                pause(dve, c_sem[0], r * 8 + (n + k), c_sem[2])
                dve.match_replace(row, top8[:, :], row, TAKEN).then_inc(c_sem[0], 1)
                pause(dve, c_sem[0], r * 8 + (n + k + 1), c_sem[2])
        n += 2 * ROUNDS
        step(dve.tensor_scalar(maskb[:, MASK_OFF[t]:MASK_OFF[t + 1]], row, -2.0e38, MASKED, ALU.is_gt, ALU.mult))


def two_layers(nc, ins, consts, out):
    ident_d, strip_d, rope_d, cos_d, sin_d = consts
    scratch = lambda name, shape, dt=F32: nc.dram_tensor(name, shape, dt, kind="Internal").ap()
    wabs_d = scratch("wabs_d", (H // 2, QC, 2 * 3 * P))
    wvo_d = scratch("wvo_d", (H // 2, P, D))
    w1T_d = scratch("w1T_d", (D, F0))
    w3T_d = scratch("w3T_d", (D, F0))
    w2T_d = scratch("w2T_d", (F0, D))
    ctx0_d = scratch("ctx0_d", (H // 2, P, S))
    ctx1_d = scratch("ctx1_d", (G1, P, S))
    qd = scratch("qd", (2, D, S))
    kvd = scratch("kvd", (2, 2 * G1 * HD1, S))
    I = lambda n: ins[n]
    with ExitStack() as top:
        c = Ctx(nc, top)
        ps = top.enter_context(nc.psum_tensor("ps", [P, 8, HALF], F32))
        ident = c.sb("ident", [P, P])
        strip = c.sb("strip", [P, S])
        x = c.sb("x", [P, ST, D])
        c_in = c.sem("c_in")
        Ctx.finished = []
        c.begin()
        with nc.Block() as block:
            @block.sync
            def _(sp):
                sp.dma_start(ident[:, :], ident_d).then_inc(c_in, 16)
                sp.dma_start(strip[:, :], strip_d).then_inc(c_in, 16)
                sp.wait_ge(c_in, START + 32)
        fold_attention_weights(nc, ps, ident, I("L0_attn_q_b_w"), I("L0_attn_kv_b_w"), I("L0_attn_o_w"), wabs_d, wvo_d)
        fold_lora(nc, ps, ident, I("L0_ffn_w1"), I("L0_ffn_w3"), I("L0_ffn_w2"), I("L0_ffn_lora_A1"),
                  I("L0_ffn_lora_B1"), I("L0_ffn_lora_A3"), I("L0_ffn_lora_B3"), I("L0_ffn_lora_A2"),
                  I("L0_ffn_lora_B2"), w1T_d, w3T_d, w2T_d)
        with ExitStack() as layer0:
            c0 = Ctx(nc, layer0)
            maskb = c0.sb("maskb", [P, MASK_OFF[ST]], BF16)
            kh = c0.sb("kh", [P, S], F32R)
            kl = c0.sb("kl", [P, S], F32R)
            vst = c0.sb("vst", [P, ST, P], F32R)
            qlh = c0.sb("qlh", [QC, 2, S], F32R)
            qll = c0.sb("qll", [QC, 2, S], F32R)
            with ExitStack() as early:
                ce = Ctx(nc, early)
                xnh = ce.sb("xnh0", [P, DT, S], F32R)
                xnl = ce.sb("xnl0", [P, DT, S], F32R)
                ikh = ce.sb("ikh", [P, S], F32R)
                ikl = ce.sb("ikl", [P, S], F32R)
                aw = ce.sb("aw", [P, ST, IH])
                sg = ce.sb("sg", [P, ST, IH])
                idx = ce.sb("idx", [P, MASK_OFF[ST]])
                top8 = ce.sb("top8", [P, 8])
                found, top_passed = ce.sem("top_step"), ce.sem("top_passed")
                ce.begin()
                layernorm(nc, "n0", ps, ident, x, xnh, xnl, I("L0_attn_hidden_states").rearrange("b s d -> (b s) d"))
                latents(nc, ps, ident, xnh, xnl, I("L0_attn_q_a_w"), I("L0_attn_kv_a_w"), I("L0_attn_idx_wk_w"),
                        I("L0_attn_idx_weights_w"), I("L0_attn_q_a_norm_w"), I("L0_attn_kv_a_norm_w"), rope_d,
                        qlh, qll, kh, kl, vst, ikh, ikl, aw, sg)
                index_scores(nc, ps, xnh, xnl, I("L0_attn_idx_wq_w"), ikh, ikl, aw, sg, idx)
                ffn(nc, "f0", ps, xnh, xnl, x, F0, w1T_d, w3T_d, w2T_d, None, None,
                    beside=lambda dve: top_keys(dve, (found, top8, top_passed), idx, maskb, strip))
                ce.finish()
            tables = (c0.sb("cosT", [P, S]), c0.sb("sinT", [P, S]))
            qwork = latent_queries(nc, ps, ident, (qlh, qll), wabs_d, cos_d, sin_d, tables)

            def passes0(i, ahead, a):
                qh, ql = qwork["bufs"]
                return [(lambda at: qh[:, a, at], lambda k0, k1: kh[:, k0:k1]),
                        (lambda at: qh[:, a, at], lambda k0, k1: kl[:, k0:k1]),
                        (lambda at: ql[:, a, at], lambda k0, k1: kh[:, k0:k1])]
            attention(nc, "a0", ps, H // 2, 2, passes0, lambda t: maskb[:, MASK_OFF[t]:MASK_OFF[t + 1]], QKD ** -0.5,
                      lambda j: vst[:, j, :], qwork, ctx0_d, 2)

            def load_wvo(sp, k, dst, sem):
                sp.dma_start(dst, wvo_d[k]).then_inc(sem, 16)
            project_out(nc, "o0", ps, x, H // 2, ctx0_d, load_wvo, 1, None)
        with ExitStack() as layer1:
            c1 = Ctx(nc, layer1)
            xnh = c1.sb("xnh1", [P, DT, S], F32R)
            xnl = c1.sb("xnl1", [P, DT, S], F32R)
            layernorm(nc, "n1", ps, ident, x, xnh, xnl)
            with ExitStack() as att:
                ca = Ctx(nc, att)
                vs_all = ca.sb("vs_all", [P, ST, G1, 2 * HD1], F32R)
                vg = ca.sb("vg", [P, ST, REP1, 2 * HD1], F32R)
                layer1_qkv(nc, ps, xnh, xnl, I("L1_attn_Wq"), I("L1_attn_Wkv"), qd, kvd, vs_all)
                qwork = stacked_queries(nc, ps, ident, vs_all, vg, qd, kvd)

                def passes1(i, ahead, a):
                    qst, kst = qwork["bufs"]
                    return [(lambda at: qst[:, a, at],
                             lambda k0, k1: kst[:, bass.ds(i + ahead, 1), k0:k1].rearrange("p o n -> p (o n)"))]
                attention(nc, "a1", ps, G1, REP1, passes1, lambda t: strip[:, S - (t + 1) * P:], HD1 ** -0.5,
                          lambda j: vg[:, j, :, :].rearrange("p r n -> p (r n)"), qwork, ctx1_d, 1)
            wo = I("L1_attn_Wo")

            def load_wo(sp, k, dst, sem):
                for h in range(REP1):
                    for l in range(2):
                        r0 = 32 * h + HD1 * l
                        sp.dma_start(dst[r0:r0 + HD1, :], wo[bass.ds(k * (REP1 * HD1) + h * HD1, HD1), :]).then_inc(sem, 16)
            project_out(nc, "o1", ps, x, G1, ctx1_d, load_wo, 2 * REP1, I("L1_attn_bo"))
            ffn(nc, "f1", ps, xnh, xnl, x, F1, I("L1_ffn_inter_w"), None, I("L1_ffn_output_w"), I("L1_ffn_inter_b"),
                I("L1_ffn_output_b"), out_d=out.rearrange("b s d -> (b s) d"))
        c.finish()
        Ctx(nc, top).begin()


_INS = ['L0_attn_hidden_states', 'L0_attn_q_a_w', 'L0_attn_q_a_norm_w', 'L0_attn_q_b_w', 'L0_attn_kv_a_w',
        'L0_attn_kv_a_norm_w', 'L0_attn_kv_b_w', 'L0_attn_o_w', 'L0_attn_idx_wq_w', 'L0_attn_idx_wk_w',
        'L0_attn_idx_weights_w', 'L0_ffn_w1', 'L0_ffn_w3', 'L0_ffn_w2', 'L0_ffn_lora_A1', 'L0_ffn_lora_B1',
        'L0_ffn_lora_A3', 'L0_ffn_lora_B3', 'L0_ffn_lora_A2', 'L0_ffn_lora_B2', 'L1_attn_Wq', 'L1_attn_Wkv',
        'L1_attn_Wo', 'L1_attn_bo', 'L1_ffn_inter_w', 'L1_ffn_inter_b', 'L1_ffn_output_w', 'L1_ffn_output_b']


def constants():
    ident = np.eye(P, dtype=np.float32)
    strip = np.zeros((P, S), np.float32)
    strip[:, S - P:] = np.where(np.arange(P)[:, None] >= np.arange(P)[None, :], 0.0, MASKED)
    inv_freq = (np.float32(1.0) / np.float32(10000.0) ** (np.arange(0, ROPE, 2, dtype=np.float32) / np.float32(ROPE)))
    ang = (np.arange(S, dtype=np.float32)[:, None] * inv_freq[None, :].astype(np.float32)).astype(np.float64)
    cos, sin = np.cos(ang).astype(np.float32), np.sin(ang).astype(np.float32)
    rope = np.stack([cos, sin], axis=1)
    cosT = np.concatenate([np.ones((64, S), np.float32), cos.T, cos.T])
    sinT = np.concatenate([-sin.T, sin.T, -sin.T, sin.T])
    return {"c_ident": ident, "c_strip": strip, "c_rope": rope, "c_cosT": cosT, "c_sinT": sinT}


def kernel(**inputs):
    import concourse.bacc as _bacc
    from concourse.bass_utils import run_bass_kernel_spmd as _run

    nc = _bacc.Bacc("TRN2", target_bir_lowering=False, num_devices=1)
    arrays, args, consts = {}, {}, []
    for name in _INS:
        a = np.ascontiguousarray(inputs[name])
        arrays[f"in_{name}"] = a
        args[name] = nc.dram_tensor(f"in_{name}", a.shape, mybir.dt.from_np(a.dtype), kind="ExternalInput").ap()
    for name, a in constants().items():
        a = np.ascontiguousarray(a)
        arrays[name] = a
        consts.append(nc.dram_tensor(name, a.shape, F32, kind="ExternalInput").ap())
    out = nc.dram_tensor("out_0_dram", (1, S, D), F32, kind="ExternalOutput").ap()
    two_layers(nc, args, consts, out)
    r = _run(nc, [arrays], core_ids=[0])
    return r.results[0]["out_0_dram"]
```
